# Optimizing a Trainium2 kernel written in Bass

```python
import numpy as np
import jax
import jax.numpy as jnp

def _softmax(x, axis=-1):
    return jax.nn.softmax(x, axis=axis)

def _gelu(x):
    return jax.nn.gelu(x, approximate=True)

def _silu(x):
    return jax.nn.silu(x)

def _sigmoid(x):
    return jax.nn.sigmoid(x)

def _layernorm(x, axis=-1, eps=1e-05):
    m = jnp.mean(x, axis=axis, keepdims=True)
    v = jnp.var(x, axis=axis, keepdims=True)
    return (x - m) / jnp.sqrt(v + eps)

def _scatter_add(tgt, idx, src, axis=0):
    return tgt.at[idx].add(src)

def _segment_sum(src, seg, n):
    return jax.ops.segment_sum(src, seg, n)
kernel_name = 'mk_flamingo_gated_d1_seqx_r4_aa0103'

def setup_inputs(seed: int=0):
    np.random.seed(seed)
    _w = jnp.asarray

    def _rec_inputs():
        import jax
        import jax.numpy as jnp
        _rk = jax.random.key(seed)
        x = 0.0003765 + 1 * jax.random.normal(jax.random.fold_in(_rk, 1), (128, 128, 256), jnp.float32)
        _lenS = 128 - jax.random.randint(jax.random.fold_in(_rk, 7), (128,), 0, max(1, 128 // 4) + 1, jnp.int32)
        _lenS2 = 128 - jax.random.randint(jax.random.fold_in(_rk, 8), (128,), 0, max(1, 128 // 4) + 1, jnp.int32)
        _ctx_1024P = jax.random.normal(jax.random.fold_in(_rk, 11), (128, 16, 256), jnp.float32)
        _ctx_1024c = jax.random.dirichlet(jax.random.fold_in(_rk, 511), 0.3 * jnp.ones((16,), jnp.float32), (128, 128))
        _ctx_1024t = jnp.einsum('bsk,bkd->bsd', _ctx_1024c, _ctx_1024P)
        _ctx_1024t = _ctx_1024t * jax.lax.rsqrt(jnp.mean(jnp.square(_ctx_1024t)) + 1e-12) * 0.953939
        ctx_1024 = -0.000292821 + 1.00034 * (_ctx_1024t + 0.3 * jax.random.normal(jax.random.fold_in(_rk, 611), (128, 128, 256), jnp.float32))
        _validS = jnp.arange(128)[None, :] < _lenS[:, None]
        _validS2 = jnp.arange(128)[None, :] < _lenS2[:, None]
        _causal = jnp.tril(jnp.ones((128, 128), dtype=bool))
        mask_1x1xSxS2_ik0 = jnp.where(jnp.broadcast_to(_validS2[0:1, None, None, :], (1, 1, 128, 128)), 0, 1).astype(jnp.int32)
        _g = jax.random.normal(jax.random.fold_in(_rk, 9001), (2, 1), jnp.float32)
        _g = jnp.sign(_g) * jnp.maximum(jnp.abs(_g), 1.0) + (_g == 0) * 1.0
        g_xattn = _g[0]
        g_ffn = _g[1]
        return (x, ctx_1024, mask_1x1xSxS2_ik0, g_xattn, g_ffn)
    x, ctx_1024, mask_1x1xSxS2_ik0, g_xattn, g_ffn = _rec_inputs()

    def _L0_xattn_setup():
        import jax, jax.numpy as jnp
        import numpy as np
        HEADS = 16
        key = jax.random.key(seed)
        ks = jax.random.split(key, 8)
        N, S, E = (2, 512, 256)
        scale = 1.0 / np.sqrt(E)
        inp = {'values': jax.random.normal(ks[0], (N, S, E), jnp.float32), 'keys': jax.random.normal(ks[1], (N, S, E), jnp.float32), 'query': jax.random.normal(ks[2], (N, S, E), jnp.float32), 'mask': jnp.tril(jnp.ones((1, 1, S, S), jnp.int32)), 'Wv': jax.random.normal(ks[3], (E, E), jnp.float32) * scale, 'bv': jnp.zeros((E,), jnp.float32), 'Wk': jax.random.normal(ks[4], (E, E), jnp.float32) * scale, 'bk': jnp.zeros((E,), jnp.float32), 'Wq': jax.random.normal(ks[5], (E, E), jnp.float32) * scale, 'bq': jnp.zeros((E,), jnp.float32), 'Wo': jax.random.normal(ks[6], (E, E), jnp.float32) * scale, 'bo': jnp.zeros((E,), jnp.float32)}
        return inp
    _L0_xattn_all = _L0_xattn_setup()
    _L0_xattn_in = {k: v for k, v in _L0_xattn_all.items() if k in ('Wv', 'bv', 'Wk', 'bk', 'Wq', 'bq', 'Wo', 'bo')}
    del _L0_xattn_all

    def _L0_ffn_setup():
        import jax, jax.numpy as jnp
        import numpy as np
        D_MODEL = 256
        key = jax.random.key(seed)
        k_x, k_w, k_a1, k_a2 = jax.random.split(key, 4)
        x = jax.random.normal(k_x, (4, 512, D_MODEL), dtype=jnp.float32)
        weight = jax.random.normal(k_w, (D_MODEL, D_MODEL), dtype=jnp.float32) * 0.02
        aux_weight1 = jax.random.normal(k_a1, (D_MODEL, D_MODEL), dtype=jnp.float32) * 0.02
        aux_weight2 = jax.random.normal(k_a2, (D_MODEL, D_MODEL), dtype=jnp.float32) * 0.02
        bias = jnp.zeros((D_MODEL,), dtype=jnp.float32)
        return {'x': x, 'weight': weight, 'aux_weight1': aux_weight1, 'aux_weight2': aux_weight2, 'bias': bias}
    _L0_ffn_all = _L0_ffn_setup()
    _L0_ffn_in = {k: v for k, v in _L0_ffn_all.items() if k in ('weight', 'aux_weight1', 'aux_weight2', 'bias')}
    del _L0_ffn_all
    return {'x': x, 'ctx_1024': ctx_1024, 'mask_1x1xSxS2_ik0': mask_1x1xSxS2_ik0, 'g_xattn': g_xattn, 'g_ffn': g_ffn, 'L0_xattn_Wv': _L0_xattn_in['Wv'], 'L0_xattn_bv': _L0_xattn_in['bv'], 'L0_xattn_Wk': _L0_xattn_in['Wk'], 'L0_xattn_bk': _L0_xattn_in['bk'], 'L0_xattn_Wq': _L0_xattn_in['Wq'], 'L0_xattn_bq': _L0_xattn_in['bq'], 'L0_xattn_Wo': _L0_xattn_in['Wo'], 'L0_xattn_bo': _L0_xattn_in['bo'], 'L0_ffn_weight': _L0_ffn_in['weight'], 'L0_ffn_aux_weight1': _L0_ffn_in['aux_weight1'], 'L0_ffn_aux_weight2': _L0_ffn_in['aux_weight2'], 'L0_ffn_bias': _L0_ffn_in['bias']}

def reference(x, ctx_1024, mask_1x1xSxS2_ik0, g_xattn, g_ffn, L0_xattn_Wv, L0_xattn_bv, L0_xattn_Wk, L0_xattn_bk, L0_xattn_Wq, L0_xattn_bq, L0_xattn_Wo, L0_xattn_bo, L0_ffn_weight, L0_ffn_aux_weight1, L0_ffn_aux_weight2, L0_ffn_bias):
    import jax
    import jax.numpy as jnp

    def _L0_xattn_ref(values, keys, query, mask, Wv, bv, Wk, bk, Wq, bq, Wo, bo):
        import jax, jax.numpy as jnp
        import numpy as np
        HEADS = 16
        N, Lq, E = query.shape
        H = HEADS
        D = E // H
        v = (values @ Wv + bv).reshape(N, -1, H, D)
        k = (keys @ Wk + bk).reshape(N, -1, H, D)
        q = (query @ Wq + bq).reshape(N, Lq, H, D)
        energy = jnp.einsum('nqhd,nkhd->nhqk', q, k)
        neg = jnp.finfo(energy.dtype).min
        energy = jnp.where(mask == 0, neg, energy)
        attn = jax.nn.softmax(energy / jnp.sqrt(jnp.asarray(D, energy.dtype)), axis=-1)
        out = jnp.einsum('nhqk,nkhd->nqhd', attn, v).reshape(N, Lq, E)
        return out @ Wo + bo

    def _L0_ffn_ref(x, weight, aux_weight1, aux_weight2, bias):
        import jax, jax.numpy as jnp
        import numpy as np
        D_MODEL = 256
        h = jnp.einsum('btc,cd->btd', x, weight)
        h = jnp.einsum('btc,cd->btd', h, aux_weight1)
        h = jnp.einsum('btc,cd->btd', h, aux_weight2)
        return jnp.tanh(h + bias)
    x = x + jnp.tanh(g_xattn[0]) * _L0_xattn_ref(ctx_1024, ctx_1024, _layernorm(x, axis=-1), mask_1x1xSxS2_ik0, L0_xattn_Wv, L0_xattn_bv, L0_xattn_Wk, L0_xattn_bk, L0_xattn_Wq, L0_xattn_bq, L0_xattn_Wo, L0_xattn_bo)
    x = x + jnp.tanh(g_ffn[0]) * _L0_ffn_ref(_layernorm(x, axis=-1), L0_ffn_weight, L0_ffn_aux_weight1, L0_ffn_aux_weight2, L0_ffn_bias)
    return x

_drawn_inputs = setup_inputs


def setup_inputs(seed=0):
    import zlib

    import numpy as np

    out = dict(_drawn_inputs(seed))
    spreads = {'L0_xattn_bv': (0.0, 0.1),
     'L0_xattn_bk': (0.0, 0.1),
     'L0_xattn_bq': (0.0, 0.1),
     'L0_xattn_bo': (0.0, 0.1),
     'L0_ffn_bias': (0.0, 0.1)}
    factors = {}
    for name, (base, spread) in spreads.items():
        noise = np.random.default_rng([zlib.crc32(name.encode()), seed]).standard_normal(out[name].shape)
        drawn = base * np.exp(spread * noise) if base else spread * noise
        out[name] = jnp.asarray(drawn.astype(out[name].dtype))
    for name, factor in factors.items():
        out[name] = (out[name] * factor).astype(out[name].dtype)
    return out
```

```python
from contextlib import ExitStack

import concourse.bass as bass
from concourse import mybir

F32 = mybir.dt.float32
BF16 = mybir.dt.bfloat16
I32 = mybir.dt.int32
ACT = mybir.ActivationFunctionType
ALU = mybir.AluOpType
AX = mybir.AxisListType

P = 128
E = 256
KT = E // P
H = 16
D = E // H
HT = P // D
G = 4
GROUPS = H // G
PAIR = 2
TOK = PAIR * P
UNITS = PAIR * GROUPS
SLOT = 32
EPS = 1e-5
MASKED = -(2.0 ** 100)
NEWTON = 1


def gated_xattn_block(nc, x, ctx, mask, g_xattn, g_ffn, Wv, bv, Wk, bk, Wq, bq, Wo, bo,
                      W1, W2, W3, b_ffn, out):
    N = x.shape[0]
    NP = N // PAIR
    BODY = 4

    x_v = x.rearrange("(p b) s e -> s p b e", b=PAIR)
    ctx_v = ctx.rearrange("(p b) s e -> s p b e", b=PAIR)
    out_v = out.rearrange("(p b) s e -> s p b e", b=PAIR)

    with ExitStack() as stack:
        def sb(name, shape, dt=F32):
            return stack.enter_context(nc.sbuf_tensor(name, shape, dt))

        def psum(name, shape):
            return stack.enter_context(nc.psum_tensor(name, shape, F32))

        def sem(name):
            return stack.enter_context(nc.semaphore(name))

        ident = sb("ident", [P, P])
        ident_h = sb("ident_h", [P, P], BF16)
        mask_i = sb("mask_i", [P, P], I32)
        mask_bias = sb("mask_bias", [P, G, P], BF16)
        wq_s, wk_s, wv_s = (sb(n, [P, KT, E]) for n in ("wq_s", "wk_s", "wv_s"))
        wo_raw, w1_s, w2_s, w3_s = (sb(n, [P, KT, E]) for n in ("wo_raw", "w1_s", "w2_s", "w3_s"))
        wo_s = sb("wo_s", [P, KT, E])
        wT_s = sb("wT_s", [P, KT, E])
        w23_s = sb("w23_s", [P, KT, E])
        wf_s = sb("wf_s", [P, KT, E])
        bq_s, bk_s, bv_s = (sb(n, [P, KT]) for n in ("bq_s", "bk_s", "bv_s"))
        bo_raw = sb("bo_raw", [1, E])
        bo_s = sb("bo_s", [1, E])
        bf_s = sb("bf_s", [1, E])
        c_zero, c_eps, c_minus_half, c_three_halves = (sb(n, [P, PAIR]) for n in (
            "c_zero", "c_eps", "c_minus_half", "c_three_halves"))
        ones_row = sb("ones_row", [1, P])
        gates = sb("gates", [P, 2])
        tgates = sb("tgates", [P, 2])

        x_in = [sb(f"x_in{i}", [P, PAIR, E]) for i in range(BODY)]
        ctx_in = [sb(f"ctx_in{i}", [P, PAIR, E]) for i in range(2)]
        xn = sb("xn", [P, PAIR, E])
        xT = sb("xT", [P, KT, TOK])
        cT = sb("cT", [P, KT, TOK])
        qT = [sb(f"qT{i}", [P, KT, TOK]) for i in range(2)]
        kT = sb("kT", [P, KT, TOK])
        k_blocks = [sb(f"k_blocks{i}", [P, KT, HT, TOK]) for i in range(2)]
        v_ones = [sb(f"v_ones{i}", [P, PAIR, H, SLOT]) for i in range(2)]
        y = [sb(f"y{i}", [P, PAIR, E]) for i in range(2)]
        yn = sb("yn", [P, PAIR, E])
        yT = sb("yT", [P, KT, TOK])
        th = sb("th", [P, PAIR, E])
        tg = sb("tg", [P, PAIR * E])
        res = [sb(f"res{i}", [P, PAIR, E]) for i in range(2)]
        stat6 = sb("stat6", [P, 2, PAIR, 6])
        stat2 = sb("stat2", [P, 2, PAIR, 2])
        ln_t = sb("ln_t", [P, 2, 6, PAIR])

        row_max = [sb(f"row_max{i}", [P, G]) for i in range(2)]
        shifted = [sb(f"shifted{i}", [P, G, P]) for i in range(2)]
        probs = [sb(f"probs{i}", [P, G, P]) for i in range(2)]
        pT = [sb(f"pT{i}", [P, G, P]) for i in range(2)]
        uT = [sb(f"uT{i}", [P, GROUPS, P]) for i in range(2)]
        den_r = [sb(f"den_r{i}", [P, H]) for i in range(2)]
        attn = [sb(f"attn{i}", [P, H, D]) for i in range(2)]
        aT = sb("aT", [P, KT, TOK])

        ps_s = [psum(f"ps_s{i}", [P, G, P]) for i in range(2)]
        ps_pT = [psum(f"ps_pT{i}", [P, G, P]) for i in range(2)]
        ps_uT = [psum(f"ps_uT{i}", [P, GROUPS, P]) for i in range(2)]
        ps_m = [psum(f"ps_m{i}", [P, 512]) for i in range(2)]

        weights_landed = sem("weights_landed")
        consts_ready = sem("consts_ready")
        setup_pe = sem("setup_pe")
        setup_act = sem("setup_act")
        setup_dve = sem("setup_dve")
        x_landed = [sem(f"x_landed{i}") for i in range(BODY)]
        ctx_landed = [sem(f"ctx_landed{i}") for i in range(2)]
        blocks_landed = [sem(f"blocks_landed{i}") for i in range(2)]
        out_stored = [sem(f"out_stored{i}") for i in range(2)]
        (stat1_ready, xn_ready, xT_done, xT_ready, cT_done, cT_ready, k_done, k_ready, q_done, q_ready,
         v_done, v_ready, s_done, shifted_ready, probs_ready, pT_done, pT_ready, pv_done, uT_ready,
         u_done, attn_ready, aT_done, aT_ready, o_done, y_ready, stat2_ready, yn_ready, yT_done, yT_ready,
         f_done, th_ready, res_ready, dve_step, pool_step, ln_constants) = (sem(n) for n in (
             "stat1_ready", "xn_ready", "xT_done", "xT_ready", "cT_done", "cT_ready", "k_done", "k_ready",
             "q_done", "q_ready", "v_done", "v_ready", "s_done", "shifted_ready", "probs_ready", "pT_done",
             "pT_ready", "pv_done", "uT_ready", "u_done", "attn_ready", "aT_done", "aT_ready", "o_done",
             "y_ready", "stat2_ready", "yn_ready", "yT_done", "yT_ready", "f_done", "th_ready", "res_ready",
             "dve_step", "pool_step", "ln_constants"))

        block = stack.enter_context(nc.Block())

        class Pair:
            def __init__(self, quot, rem):
                self.quot, self.rem = quot + rem // BODY if rem // BODY else quot, rem % BODY
                self.n = self.quot * BODY + self.rem if self.rem else self.quot * BODY
                self.known = isinstance(self.n, int)

            def times(self, per, plus):
                return self.quot * (BODY * per) + (self.rem * per + plus)

            def lap(self, ring, per):
                return self.quot * (BODY // ring * per) + (self.rem // ring + 1) * per

            def back(self, k):
                return Pair(self.quot, self.rem - k)

            def exists(self):
                return not self.known or 0 <= self.n < NP

        def turns(eng, body, first=0):
            for t in range(BODY):
                body(Pair(0, t))
            with eng.Fori(1, NP // BODY) as i:
                for r in range(BODY):
                    body(Pair(i, r))
            for t in range(NP, NP + 2):
                body(Pair(t // BODY, t % BODY))

        def wait(eng, semaphore, value):
            if not isinstance(value, int) or value > 0:
                eng.wait_ge(semaphore, value)

        @block.sync
        def _(sp):
            for dst, src in ((wq_s, Wq), (wk_s, Wk), (wv_s, Wv), (wo_raw, Wo), (w1_s, W1), (w2_s, W2), (w3_s, W3)):
                sp.dma_start(dst[:], src.rearrange("(k p) n -> p k n", p=P)).then_inc(weights_landed, 16)
            for dst, src in ((bq_s, bq), (bk_s, bk), (bv_s, bv)):
                sp.dma_start(dst[:], src.rearrange("(k p) -> p k", p=P), allow_slow_non_contiguous=True).then_inc(weights_landed, 16)
            for dst, src in ((bo_raw, bo), (bf_s, b_ffn)):
                sp.dma_start(dst[:], src.rearrange("(a n) -> a n", a=1)).then_inc(weights_landed, 16)
            for j, src in enumerate((g_xattn, g_ffn)):
                sp.dma_start(gates[:, j:j + 1], src.rearrange("(a n) -> a n", a=1).to_broadcast([P, 1])).then_inc(weights_landed, 16)
            sp.dma_start(mask_i[:], mask[0, 0]).then_inc(weights_landed, 16)

            def early(value, most):
                return value if isinstance(value, int) else sp.snap(value, min_val=0, max_val=most)

            def load(p):
                n = early(p.n, NP - 1)
                x_free, ctx_free = early(p.times(1, -3), NP), early(p.times(1, -1), NP)
                wait(sp, y_ready, x_free)
                sp.dma_start(x_in[p.rem][:], x_v[:, bass.ds(n, 1)].rearrange("s p b e -> s (p b) e")).then_inc(x_landed[p.rem], 16)
                wait(sp, cT_done, ctx_free)
                sp.dma_start(ctx_in[p.rem % 2][:], ctx_v[:, bass.ds(n, 1)].rearrange("s p b e -> s (p b) e")).then_inc(ctx_landed[p.rem % 2], 16)

            def spread(p):
                sp.wait_ge(k_ready, p.times(1, 1))
                for m in range(KT):
                    for h in range(HT):
                        sp.dma_start(k_blocks[p.rem % 2][h * D:(h + 1) * D, m, h, :],
                                     kT[h * D:(h + 1) * D, m, :]).then_inc(blocks_landed[p.rem % 2], 16)

            def store(p):
                n, written = early(p.n, NP - 1), early(p.times(1, 1), NP)
                sp.wait_ge(res_ready, written)
                sp.dma_start(out_v[:, bass.ds(n, 1)].rearrange("s p b e -> s (p b) e"), res[p.rem % 2][:]).then_inc(out_stored[p.rem % 2], 16)

            def body(t):
                if t.known and t.n == 0:
                    load(t)
                if t.back(-1).exists():
                    load(t.back(-1))
                if t.exists():
                    spread(t)
                if t.back(2).exists():
                    store(t.back(2))

            for t in range(BODY):
                body(Pair(0, t))
            with sp.Fori(1, NP // BODY - 1) as i:
                for r in range(BODY):
                    body(Pair(i, r))
            for t in range(NP - BODY, NP + 2):
                body(Pair(t // BODY, t % BODY))
            for o in out_stored:
                sp.wait_ge(o, 16 * (NP // 2))

        @block.gpsimd
        def _(pool):
            nc.gpsimd.memset(ident[:], 0.0).then_inc(consts_ready, 1)
            nc.gpsimd.memset(ident_h[:], 0.0).then_inc(consts_ready, 1)
            for tile, value in ((c_zero, 0.0), (c_eps, EPS), (c_minus_half, -0.5), (c_three_halves, 1.5)):
                nc.gpsimd.memset(tile[:], value)
            nc.gpsimd.memset(ones_row[:], 1.0).then_inc(consts_ready, 1)
            pool.wait_ge(consts_ready, 3)
            for m in (ident, ident_h):
                nc.gpsimd.affine_select(out=m[:], in_=m[:], compare_op=ALU.not_equal, fill=1.0, base=0,
                                        pattern=[[-1, P]], channel_multiplier=1).then_inc(consts_ready, 1)
            for i in range(2):
                nc.gpsimd.memset(k_blocks[i][:].rearrange("p a b c -> p (a b c)"), 0.0).then_inc(consts_ready, 1)
                nc.gpsimd.memset(v_ones[i][:].rearrange("p a b c -> p (a b c)"), 1.0).then_inc(consts_ready, 1)

            def rstd(which, before):
                vp, r, a, b, nm = (ln_t[:, which, j, :] for j in range(5))
                mean, var = stat2[:, which, :, 0], stat2[:, which, :, 1]
                done = [0]

                def step(out, in0, in1, op):
                    nc.gpsimd.tensor_tensor(out, in0, in1, op).then_inc(pool_step, 1)
                    done[0] += 1
                    pool.wait_ge(pool_step, before + done[0])

                step(vp, var, c_eps[:], ALU.add)
                step(r, vp, c_minus_half[:], ALU.pow)
                for _ in range(NEWTON):
                    step(a, r, r, ALU.mult)
                    step(b, a, vp, ALU.mult)
                    step(a, b, c_minus_half[:], ALU.mult)
                    step(b, a, c_three_halves[:], ALU.add)
                    step(r, r, b, ALU.mult)
                step(a, mean, r, ALU.mult)
                step(nm, c_zero[:], a, ALU.subtract)
                pool.sem_inc(ln_constants, 1)
                assert done[0] == per_ln

            per_ln = 2 + 5 * NEWTON + 2

            def normalise(which, dst, src, ready):
                for b in range(PAIR):
                    last = nc.gpsimd.tensor_scalar(dst[:, b, :], src[:, b, :], ln_t[:, which, 1, b:b + 1],
                                                   ln_t[:, which, 4, b:b + 1], ALU.mult, ALU.add)
                    last.then_inc(ready, 1)

            STEPS_A, STEPS_C = per_ln, per_ln + 1

            def body(t):
                c = t.back(2)
                if t.known:
                    before_1 = STEPS_A * min(t.n, NP) + STEPS_C * max(0, t.n - 2)
                    before_2 = before_1 + (STEPS_A if t.exists() else 0)
                else:
                    before_1 = t.times(STEPS_A + STEPS_C, -2 * STEPS_C)
                    before_2 = t.times(STEPS_A + STEPS_C, STEPS_A - 2 * STEPS_C)
                if t.exists():
                    pool.wait_ge(stat1_ready, t.times(1, 1))
                    wait(pool, xT_done, t.times(1, 0))
                    pool.wait_ge(x_landed[t.rem], t.lap(BODY, 16))
                    rstd(0, before_1)
                    normalise(0, xn, x_in[t.rem], xn_ready)
                if c.exists():
                    pool.wait_ge(stat2_ready, c.times(1, 1))
                    wait(pool, yT_done, c.times(1, 0))
                    pool.wait_ge(y_ready, c.times(1, 1))
                    rstd(1, before_2)
                    normalise(1, yn, y[c.rem % 2], yn_ready)
                    pool.wait_ge(th_ready, c.times(1, 1))
                    nc.gpsimd.tensor_tensor(tg[:], th[:].rearrange("p b e -> p (b e)"), tgates[:, 1:2].to_broadcast([P, PAIR * E]),
                                            ALU.mult).then_inc(pool_step, 1)
                    pool.wait_ge(pool_step, before_2 + STEPS_C)
                    wait(pool, out_stored[c.rem % 2], c.lap(2, 16) - 16)
                    nc.gpsimd.tensor_tensor(res[c.rem % 2][:].rearrange("p b e -> p (b e)"), tg[:],
                                            y[c.rem % 2][:].rearrange("p b e -> p (b e)"), ALU.add).then_inc(res_ready, 1)

            pool.wait_ge(setup_act, 1)
            turns(pool, body)

        MISC = [("u0", 0), ("xT", 1), ("u1", 0), ("cT", 1), ("aT", 0), ("k", 1), ("o", 0), ("q", 1), ("v", 0), ("yT", 1), ("f", 0)]

        @block.tensor
        def _(pe):
            read_by = {"u0": (attn_ready, 2, 1, 2), "u1": (attn_ready, 2, 2, 2), "xT": (xT_ready, 1, 1, 0), "cT": (cT_ready, 1, 1, 0),
                       "aT": (aT_ready, 1, 1, 2), "k": (k_ready, 2, 2, 0), "o": (y_ready, 1, 1, 2), "q": (q_ready, 2, 2, 0),
                       "v": (v_ready, 1, 1, 0), "yT": (yT_ready, 1, 1, 2), "f": (th_ready, 1, 1, 2)}
            read_by["k"] = (k_ready, 1, 1, 0)
            read_by["q"] = (q_ready, 1, 1, 0)

            def bank_of(name, t):
                at = [n for n, _ in MISC].index(name)
                bank = MISC[at][1]
                k, turn = at, t
                while True:
                    k -= 1
                    if k < 0:
                        k, turn = len(MISC) - 1, turn.back(1)
                    if turn.known and turn.n < 0:
                        return ps_m[bank]
                    other, b = MISC[k]
                    semaphore, per, nth, lag = read_by[other]
                    if b == bank and turn.back(lag).exists():
                        pe.wait_ge(semaphore, turn.back(lag).times(per, nth))
                        return ps_m[bank]

            def transposes(dst, src):
                for k in range(KT):
                    for b in range(PAIR):
                        last = nc.tensor.transpose(dst[:, k * TOK + b * P:k * TOK + (b + 1) * P], src[b][:, k * P:(k + 1) * P], ident[:])
                return last

            def project_T(dst, w, src):
                for m in range(KT):
                    for k in range(KT):
                        last = nc.tensor.matmul(dst[:, m * TOK:(m + 1) * TOK], w[:, k, m * P:(m + 1) * P], src[:, k, :],
                                                start=(k == 0), stop=(k == KT - 1))
                return last

            def project(dst, src, w, bias=None):
                for b in range(PAIR):
                    o = dst[:, b * E:(b + 1) * E]
                    if bias is not None:
                        nc.tensor.matmul(o, ones_row[:], bias[:], start=True, stop=False)
                    for k in range(KT):
                        last = nc.tensor.matmul(o, src[:, k, b * P:(b + 1) * P], w[:, k, :],
                                                start=(k == 0 and bias is None), stop=(k == KT - 1))
                return last

            def setup():
                pe.wait_ge(weights_landed, 16 * 15)
                pe.wait_ge(consts_ready, 9)

                def transpose_w(w):
                    for k in range(KT):
                        for j in range(KT):
                            last = nc.tensor.transpose(ps_m[0][:, j * E + k * P:j * E + (k + 1) * P], w[:, k, j * P:(j + 1) * P], ident[:])
                    last.then_inc(setup_pe, 1)

                def product(rhs):
                    for m in range(KT):
                        for k in range(KT):
                            last = nc.tensor.matmul(ps_m[1][:, m * E:(m + 1) * E], wT_s[:, k, m * P:(m + 1) * P], rhs[:, k, :],
                                                    start=(k == 0), stop=(k == KT - 1))
                    last.then_inc(setup_pe, 1)

                transpose_w(w2_s)
                pe.wait_ge(setup_dve, 2)
                product(w3_s)
                pe.wait_ge(setup_dve, 3)
                transpose_w(w1_s)
                pe.wait_ge(setup_dve, 4)
                product(w23_s)
                pe.wait_ge(setup_dve, 5)
                o = ps_m[0][0:1, 0:E]
                nc.tensor.matmul(o, ones_row[0:1, 0:1], bo_raw[:], start=True, stop=False)
                for k in range(KT):
                    last = nc.tensor.matmul(o, bv_s[:, k:k + 1], wo_raw[:, k, :], start=False, stop=(k == KT - 1))
                last.then_inc(setup_pe, 1)
                pe.wait_ge(setup_dve, 7)

            def scores(b, u):
                n, g = u // GROUPS, u % GROUPS
                m, h0 = g * G // HT, g * G % HT
                if u == 0:
                    pe.wait_ge(q_ready, b.times(1, 1))
                    pe.wait_ge(blocks_landed[b.rem % 2], b.lap(2, 16 * H))
                wait(pe, shifted_ready, b.times(UNITS, u - 1))
                s = ps_s[u % 2]
                nc.tensor.matmul(s[:], ident_h[:], mask_bias[:], start=True, stop=False)
                nc.tensor.matmul(s[:], qT[b.rem % 2][:, m, n * P:(n + 1) * P],
                                 k_blocks[b.rem % 2][:, m, h0:h0 + G, n * P:(n + 1) * P],
                                 start=False, stop=True).then_inc(s_done, 1)

            def transpose_probs(b, u):
                pe.wait_ge(probs_ready, b.times(UNITS, u + 1))
                wait(pe, pT_ready, b.times(UNITS, u - 1))
                for h in range(G):
                    last = nc.tensor.transpose(ps_pT[u % 2][:, h, :], probs[u % 2][:, h, :], ident[:])
                last.then_inc(pT_done, 1)

            def weigh_values(b, u):
                n, g = u // GROUPS, u % GROUPS
                if u == 0:
                    pe.wait_ge(v_ready, b.times(1, 1))
                if g == 0:
                    wait(pe, uT_ready, b.times(PAIR, n - 1))
                pe.wait_ge(pT_ready, b.times(UNITS, u + 1))
                for h in range(G):
                    last = nc.tensor.matmul(ps_uT[n][h * SLOT:(h + 1) * SLOT, g, :], v_ones[b.rem % 2][:, n, g * G + h, :],
                                            pT[u % 2][:, h, :], start=True, stop=True, tile_position=(0, h * SLOT))
                last.then_inc(pv_done, 1)

            def untranspose(c, n):
                dst = bank_of(f"u{n}", c.back(-2))
                pe.wait_ge(uT_ready, c.times(PAIR, n + 1))
                for g in range(GROUPS):
                    last = nc.tensor.transpose(dst[:, g * P:(g + 1) * P], uT[n][:, g, :], ident[:])
                last.then_inc(u_done, 1)

            def body(t):
                b, c = t.back(1), t.back(2)
                A, B, C = t.exists(), b.exists(), c.exists()

                def attend(u):
                    if B:
                        transpose_probs(b, u)
                    if u > 0 and B:
                        weigh_values(b, u - 1)
                    if u == 0 and C:
                        weigh_values(c, UNITS - 1)

                def ahead(u):
                    if B and u < UNITS:
                        scores(b, u)

                ahead(1)
                if C:
                    untranspose(c, 0)
                if A:
                    dst = bank_of("xT", t)
                    pe.wait_ge(xn_ready, t.times(PAIR, PAIR))
                    transposes(dst, [xn[:, i, :] for i in range(PAIR)]).then_inc(xT_done, 1)
                attend(0)

                ahead(2)
                if C:
                    untranspose(c, 1)
                attend(1)

                ahead(3)
                if A:
                    dst = bank_of("cT", t)
                    pe.wait_ge(ctx_landed[t.rem % 2], t.lap(2, 16))
                    transposes(dst, [ctx_in[t.rem % 2][:, i, :] for i in range(PAIR)]).then_inc(cT_done, 1)
                attend(2)

                ahead(4)
                if C:
                    dst = bank_of("aT", t)
                    pe.wait_ge(attn_ready, c.times(PAIR, PAIR))
                    transposes(dst, [attn[i][:].rearrange("p h d -> p (h d)") for i in range(PAIR)]).then_inc(aT_done, 1)
                if A:
                    dst = bank_of("k", t)
                    pe.wait_ge(cT_ready, t.times(1, 1))
                    project_T(dst, wk_s, cT).then_inc(k_done, 1)
                attend(3)

                ahead(5)
                if C:
                    dst = bank_of("o", t)
                    pe.wait_ge(aT_ready, c.times(1, 1))
                    project(dst, aT, wo_s, bo_s).then_inc(o_done, 1)
                if A:
                    dst = bank_of("q", t)
                    pe.wait_ge(xT_ready, t.times(1, 1))
                    project_T(dst, wq_s, xT).then_inc(q_done, 1)
                attend(4)

                ahead(6)
                if A:
                    dst = bank_of("v", t)
                    project(dst, cT, wv_s).then_inc(v_done, 1)
                attend(5)

                ahead(7)
                if C:
                    dst = bank_of("yT", t)
                    pe.wait_ge(yn_ready, c.times(PAIR, PAIR))
                    transposes(dst, [yn[:, i, :] for i in range(PAIR)]).then_inc(yT_done, 1)
                attend(6)

                if A:
                    scores(t, 0)
                if C:
                    dst = bank_of("f", t)
                    pe.wait_ge(yT_ready, c.times(1, 1))
                    project(dst, yT, wf_s, bf_s).then_inc(f_done, 1)
                attend(7)

            setup()
            turns(pe, body)

        @block.scalar
        def _(act):
            act.wait_ge(weights_landed, 16 * 15)
            nc.scalar.activation(tgates[:], gates[:], ACT.Tanh).then_inc(setup_act, 1)

            def flat(a):
                return a[:].rearrange("p a b -> p (a b)")

            def copy(dst, src, ready):
                nc.scalar.activation(dst, src, ACT.Copy).then_inc(ready, 1)

            def expo(b, u):
                act.wait_ge(shifted_ready, b.times(UNITS, u + 1))
                wait(act, pT_done, b.times(UNITS, u - 1))
                nc.scalar.activation(flat(probs[u % 2]), flat(shifted[u % 2]), ACT.Exp,
                                     scale=float(D) ** -0.5).then_inc(probs_ready, 1)

            def copy_pT(b, u):
                act.wait_ge(pT_done, b.times(UNITS, u + 1))
                wait(act, pv_done, b.times(UNITS, u - 1))
                copy(flat(pT[u % 2]), flat(ps_pT[u % 2]), pT_ready)

            def copy_uT(b, n):
                act.wait_ge(pv_done, b.times(UNITS, (n + 1) * GROUPS))
                wait(act, u_done, b.times(PAIR, n - 1))
                copy(flat(uT[n]), flat(ps_uT[n]), uT_ready)

            def body(t):
                b, c = t.back(1), t.back(2)
                A, B, C = t.exists(), b.exists(), c.exists()

                def attend(u):
                    if B:
                        expo(b, u)
                        copy_pT(b, u)

                attend(0)
                if C:
                    copy_uT(c, 1)
                if A:
                    act.wait_ge(xT_done, t.times(1, 1))
                    wait(act, q_done, t.times(1, 0))
                    copy(flat(xT), ps_m[1][:], xT_ready)
                attend(1)
                attend(2)
                if A:
                    act.wait_ge(cT_done, t.times(1, 1))
                    wait(act, v_done, t.times(1, 0))
                    copy(flat(cT), ps_m[1][:], cT_ready)
                attend(3)
                if C:
                    act.wait_ge(aT_done, c.times(1, 1))
                    wait(act, o_done, c.times(1, 0))
                    copy(flat(aT), ps_m[0][:], aT_ready)
                if A:
                    act.wait_ge(k_done, t.times(1, 1))
                    wait(act, s_done, t.times(UNITS, -UNITS))
                    if not t.known or t.n > 0:
                        act.wait_ge(blocks_landed[(t.rem - 1) % 2], t.back(1).lap(2, 16 * H))
                    for m in range(KT):
                        last = nc.scalar.activation(kT[:, m, :], ps_m[1][:, m * TOK:(m + 1) * TOK], ACT.Identity, bias=bk_s[:, m:m + 1])
                    last.then_inc(k_ready, 1)
                attend(4)
                if B:
                    copy_uT(b, 0)
                if A:
                    act.wait_ge(q_done, t.times(1, 1))
                    for m in range(KT):
                        last = nc.scalar.activation(qT[t.rem % 2][:, m, :], ps_m[1][:, m * TOK:(m + 1) * TOK], ACT.Identity, bias=bq_s[:, m:m + 1])
                    last.then_inc(q_ready, 1)
                attend(5)
                if A:
                    act.wait_ge(v_done, t.times(1, 1))
                    wait(act, pv_done, t.times(UNITS, -UNITS))
                    nc.scalar.activation(v_ones[t.rem % 2][:, :, :, 0:D],
                                         ps_m[0][:].rearrange("p (b h d) -> p b h d", b=PAIR, d=D), ACT.Copy).then_inc(v_ready, 1)
                attend(6)
                if C:
                    act.wait_ge(yT_done, c.times(1, 1))
                    wait(act, f_done, c.times(1, 0))
                    copy(flat(yT), ps_m[1][:], yT_ready)
                attend(7)
                if C:
                    act.wait_ge(f_done, c.times(1, 1))
                    wait(act, res_ready, c.times(1, 0))
                    nc.scalar.activation(flat(th), ps_m[0][:], ACT.Tanh).then_inc(th_ready, 1)

            turns(act, body)

        @block.vector
        def _(dve):
            dve.wait_ge(weights_landed, 16 * 15)
            for h in range(G):
                last = nc.vector.tensor_scalar(mask_bias[:, h, :], mask_i[:], 0, MASKED, ALU.is_equal, ALU.mult)
            last.then_inc(setup_dve, 1)
            for n, (dst, bank) in enumerate(((wT_s, 0), (w23_s, 1), (wT_s, 0), (wf_s, 1))):
                dve.wait_ge(setup_pe, n + 1)
                nc.vector.tensor_copy(dst[:].rearrange("p k n -> p (k n)"), ps_m[bank][:]).then_inc(setup_dve, 1)
            dve.wait_ge(setup_pe, 5)
            dve.wait_ge(setup_act, 1)
            nc.vector.tensor_scalar(bo_s[:], ps_m[0][0:1, 0:E], tgates[0:1, 0:1], None, ALU.mult).then_inc(setup_dve, 1)
            nc.vector.tensor_scalar(wo_s[:].rearrange("p k n -> p (k n)"), wo_raw[:].rearrange("p k n -> p (k n)"),
                                    tgates[:, 0:1], None, ALU.mult).then_inc(setup_dve, 1)

            STEPS_A, STEPS_B, STEPS_C = 1, UNITS, 1 + PAIR

            def body(t):
                b, c = t.back(1), t.back(2)
                A, B, C = t.exists(), b.exists(), c.exists()
                done = [0]
                if t.known:
                    before = STEPS_A * min(t.n, NP) + STEPS_B * max(0, t.n - 1) + STEPS_C * max(0, t.n - 2)
                else:
                    before = t.times(STEPS_A + STEPS_B + STEPS_C, -STEPS_B - 2 * STEPS_C)

                def step(inst):
                    inst.then_inc(dve_step, 1)
                    done[0] += 1
                    dve.wait_ge(dve_step, before + done[0])


                def soften(u, stats=None):
                    if stats is not None:
                        which, src, ready = stats
                        for i in range(PAIR):
                            last = nc.vector.bn_stats(stat6[:, which, i, :], src[:, i, :])
                        last.then_inc(dve_step, 1)
                        done[0] += 1
                        if not B:
                            dve.wait_ge(dve_step, before + done[0])
                    if B:
                        maximum(u)
                    if stats is not None:
                        for i in range(PAIR):
                            last = nc.vector.bn_aggr(stat2[:, which, i, :], stat6[:, which, i, :])
                        last.then_inc(ready, 1)

                def maximum(u):
                    dve.wait_ge(s_done, b.times(UNITS, u + 1))
                    step(nc.vector.tensor_reduce(row_max[u % 2][:], ps_s[u % 2][:], axis=AX.X, op=ALU.max))
                    wait(dve, probs_ready, b.times(UNITS, u - 1))
                    nc.vector.tensor_tensor(shifted[u % 2][:], ps_s[u % 2][:], row_max[u % 2][:].unsqueeze(2).to_broadcast([P, G, P]),
                                            ALU.subtract).then_inc(shifted_ready, 1)

                def normalise(n):
                    if not C:
                        return
                    dve.wait_ge(u_done, c.times(PAIR, n + 1))
                    u = ps_m[0][:].rearrange("p (h s) -> p h s", s=SLOT)
                    step(nc.vector.reciprocal(den_r[n][:], u[:, :, D]))
                    wait(dve, aT_done, c.times(1, 0))
                    nc.vector.tensor_tensor(attn[n][:], u[:, :, 0:D], den_r[n][:].unsqueeze(2).to_broadcast([P, H, D]),
                                            ALU.mult).then_inc(attn_ready, 1)

                stats_1 = stats_2 = None
                if A:
                    dve.wait_ge(x_landed[t.rem], t.lap(BODY, 16))
                    wait(dve, xn_ready, t.times(PAIR, 0))
                    stats_1 = (0, x_in[t.rem], stat1_ready)
                for u in range(UNITS):
                    if u == 5 and C:
                        yy = y[c.rem % 2]
                        wait(dve, yn_ready, c.times(PAIR, 0))
                        dve.wait_ge(y_ready, c.times(1, 1))
                        stats_2 = (1, yy, stat2_ready)
                    soften(u, {0: stats_1, 5: stats_2}.get(u))
                    if u < PAIR:
                        normalise(u)
                    if u == 4 and C:
                        dve.wait_ge(o_done, c.times(1, 1))
                        wait(dve, res_ready, c.times(1, -1))
                        nc.vector.tensor_tensor(y[c.rem % 2][:].rearrange("p b e -> p (b e)"), ps_m[0][:],
                                                x_in[c.rem][:].rearrange("p b e -> p (b e)"), ALU.add).then_inc(y_ready, 1)

            turns(dve, body)


_INS = ["x", "ctx_1024", "mask_1x1xSxS2_ik0", "g_xattn", "g_ffn", "L0_xattn_Wv", "L0_xattn_bv", "L0_xattn_Wk",
        "L0_xattn_bk", "L0_xattn_Wq", "L0_xattn_bq", "L0_xattn_Wo", "L0_xattn_bo", "L0_ffn_weight",
        "L0_ffn_aux_weight1", "L0_ffn_aux_weight2", "L0_ffn_bias"]


def kernel(**inputs):
    import numpy as np
    import concourse.bacc as bacc
    from concourse.bass_utils import run_bass_kernel_spmd

    nc = bacc.Bacc("TRN2", target_bir_lowering=False, num_devices=1)
    arrays, args = {}, []
    for name in _INS:
        a = np.ascontiguousarray(inputs[name])
        arrays[f"in_{name}"] = a
        args.append(nc.dram_tensor(f"in_{name}", a.shape, mybir.dt.from_np(a.dtype), kind="ExternalInput").ap())
    shape = np.shape(inputs["x"])
    args.append(nc.dram_tensor("out_0", shape, F32, kind="ExternalOutput").ap())
    gated_xattn_block(nc, *args)
    r = run_bass_kernel_spmd(nc, [arrays], core_ids=[0])
    return r.results[0]["out_0"]
```

```python
from contextlib import ExitStack

import concourse.bass as bass
from concourse import mybir

F32 = mybir.dt.float32
F32R = mybir.dt.float32r
BF16 = mybir.dt.bfloat16
I32 = mybir.dt.int32
ACT = mybir.ActivationFunctionType
ALU = mybir.AluOpType
AX = mybir.AxisListType

P = 128
E = 256
KT = E // P
H = 16
D = E // H
HT = P // D
G = 4
GROUPS = H // G
PAIR = 2
TOK = PAIR * P
UNITS = PAIR * GROUPS
SLOT = 32
EPS = 1e-5
MASKED = -(2.0 ** 100)
NEWTON = 1


def gated_xattn_block(nc, x, ctx, mask, g_xattn, g_ffn, Wv, bv, Wk, bk, Wq, bq, Wo, bo,
                      W1, W2, W3, b_ffn, out):
    N = x.shape[0]
    NP = N // PAIR
    BODY = 4

    x_v = x.rearrange("(p b) s e -> s p b e", b=PAIR)
    ctx_v = ctx.rearrange("(p b) s e -> s p b e", b=PAIR)
    out_v = out.rearrange("(p b) s e -> s p b e", b=PAIR)

    with ExitStack() as stack:
        def sb(name, shape, dt=F32):
            return stack.enter_context(nc.sbuf_tensor(name, shape, dt))

        def psum(name, shape):
            return stack.enter_context(nc.psum_tensor(name, shape, F32))

        def sem(name):
            return stack.enter_context(nc.semaphore(name))

        ident = sb("ident", [P, P])
        ident_h = sb("ident_h", [P, P], BF16)
        mask_i = sb("mask_i", [P, P], I32)
        mask_bias = sb("mask_bias", [P, G, P], BF16)
        wq_raw, wk_raw, wv_raw = (sb(n, [P, KT, E]) for n in ("wq_raw", "wk_raw", "wv_raw"))
        wq_s, wk_s, wv_s, wo_s, wf_s = (sb(n, [P, 2, KT, E], F32R) for n in ("wq_s", "wk_s", "wv_s", "wo_s", "wf_s"))
        wo_raw, w1_s, w2_s, w3_s = (sb(n, [P, KT, E]) for n in ("wo_raw", "w1_s", "w2_s", "w3_s"))
        wo_g = sb("wo_g", [P, KT, E])
        wT_s = sb("wT_s", [P, KT, E])
        w23_s = sb("w23_s", [P, KT, E])
        w123_s = sb("w123_s", [P, KT, E])
        bq_s, bk_s, bv_s = (sb(n, [P, KT]) for n in ("bq_s", "bk_s", "bv_s"))
        bo_raw = sb("bo_raw", [1, E])
        bo_g = sb("bo_g", [1, E])
        bf_raw = sb("bf_raw", [1, E])
        bias_low = sb("bias_low", [1, 2, E], F32R)
        bias_rows = [sb(f"bias_rows{i}", [P, E], F32R) for i in range(2)]
        ones_sq = sb("ones_sq", [P, P], F32R)
        c_zero, c_eps, c_minus_half, c_three_halves = (sb(n, [P, PAIR]) for n in (
            "c_zero", "c_eps", "c_minus_half", "c_three_halves"))
        ones_row = sb("ones_row", [1, P])
        gates = sb("gates", [P, 2])
        tgates = sb("tgates", [P, 2])

        x_in = [sb(f"x_in{i}", [P, PAIR, E]) for i in range(BODY)]
        ctx_in = [sb(f"ctx_in{i}", [P, PAIR, E]) for i in range(2)]
        xn = sb("xn", [P, PAIR, E])
        xT = sb("xT", [P, 2, KT, TOK], F32R)
        cT = sb("cT", [P, 2, KT, TOK], F32R)
        qT = [sb(f"qT{i}", [P, 2, KT, TOK], F32R) for i in range(2)]
        kT = sb("kT", [P, 2, KT, TOK], F32R)
        k_blocks = [sb(f"k_blocks{i}", [P, 2 * KT, HT, TOK], F32R) for i in range(2)]
        v_ones = [sb(f"v_ones{i}", [P, PAIR, H, SLOT]) for i in range(2)]
        y = [sb(f"y{i}", [P, PAIR, E]) for i in range(2)]
        yn = sb("yn", [P, PAIR, E])
        yT = sb("yT", [P, 2, KT, TOK], F32R)
        th = sb("th", [P, PAIR, E])
        tg = sb("tg", [P, PAIR * E])
        res = [sb(f"res{i}", [P, PAIR, E]) for i in range(2)]
        stat6 = sb("stat6", [P, 2, PAIR, 6])
        stat2 = sb("stat2", [P, 2, PAIR, 2])
        ln_t = sb("ln_t", [P, 2, 6, PAIR])

        row_max = [sb(f"row_max{i}", [P, G]) for i in range(2)]
        shifted = [sb(f"shifted{i}", [P, G, P]) for i in range(2)]
        probs = [sb(f"probs{i}", [P, G, P]) for i in range(2)]
        pT = [sb(f"pT{i}", [P, G, P]) for i in range(2)]
        uT = [sb(f"uT{i}", [P, GROUPS, P]) for i in range(2)]
        den_r = [sb(f"den_r{i}", [P, H]) for i in range(2)]
        attn = [sb(f"attn{i}", [P, H, D]) for i in range(2)]
        aT = sb("aT", [P, 2, KT, TOK], F32R)

        ps_s = [psum(f"ps_s{i}", [P, G, P]) for i in range(2)]
        ps_pT = [psum(f"ps_pT{i}", [P, G, P]) for i in range(2)]
        ps_uT = psum("ps_uT", [P, GROUPS, P])
        ps_m = [psum(f"ps_m{i}", [P, 512]) for i in range(3)]
        STEPS = ("u0", "xT", "u1", "cT", "aT", "k", "o", "q", "v", "yT", "f")
        BANK = {name: i % len(ps_m) for i, name in enumerate(STEPS)}

        weights_landed = sem("weights_landed")
        consts_ready = sem("consts_ready")
        setup_pe = sem("setup_pe")
        setup_act = sem("setup_act")
        setup_dve = sem("setup_dve")
        x_landed = [sem(f"x_landed{i}") for i in range(BODY)]
        ctx_landed = [sem(f"ctx_landed{i}") for i in range(2)]
        blocks_landed = [sem(f"blocks_landed{i}") for i in range(2)]
        out_stored = [sem(f"out_stored{i}") for i in range(2)]
        (stat1_ready, xn_ready, xT_done, xT_ready, cT_done, cT_ready, k_done, k_ready, q_done, q_ready,
         v_done, v_ready, s_done, shifted_ready, probs_ready, pT_done, pT_ready, pv_done, uT_ready,
         u_done, attn_ready, aT_done, aT_ready, o_done, y_ready, stat2_ready, yn_ready, yT_done, yT_ready,
         f_done, th_ready, res_ready, dve_step, pool_step, ln_constants,
         xT_high, cT_high, k_high, q_high, aT_high, yT_high, bias_landed) = (sem(n) for n in (
             "stat1_ready", "xn_ready", "xT_done", "xT_ready", "cT_done", "cT_ready", "k_done", "k_ready",
             "q_done", "q_ready", "v_done", "v_ready", "s_done", "shifted_ready", "probs_ready", "pT_done",
             "pT_ready", "pv_done", "uT_ready", "u_done", "attn_ready", "aT_done", "aT_ready", "o_done",
             "y_ready", "stat2_ready", "yn_ready", "yT_done", "yT_ready", "f_done", "th_ready", "res_ready",
             "dve_step", "pool_step", "ln_constants", "xT_high", "cT_high", "k_high", "q_high", "aT_high", "yT_high",
             "bias_landed"))

        BIAS_SPLIT, WEIGHTS_SPLIT = 9, 10

        block = stack.enter_context(nc.Block())

        class Pair:
            def __init__(self, quot, rem):
                self.quot, self.rem = quot + rem // BODY if rem // BODY else quot, rem % BODY
                self.n = self.quot * BODY + self.rem if self.rem else self.quot * BODY
                self.known = isinstance(self.n, int)

            def times(self, per, plus):
                return self.quot * (BODY * per) + (self.rem * per + plus)

            def lap(self, ring, per):
                return self.quot * (BODY // ring * per) + (self.rem // ring + 1) * per

            def back(self, k):
                return Pair(self.quot, self.rem - k)

            def exists(self):
                return not self.known or 0 <= self.n < NP

        def turns(eng, body):
            for t in range(BODY):
                body(Pair(0, t))
            with eng.Fori(1, NP // BODY - 1) as i:
                for r in range(BODY):
                    body(Pair(i, r))
            for t in range(NP - BODY, NP + 2):
                body(Pair(t // BODY, t % BODY))

        def wait(eng, semaphore, value):
            if not isinstance(value, int) or value > 0:
                eng.wait_ge(semaphore, value)

        @block.sync
        def _(sp):
            for dst, src in ((wq_raw, Wq), (wk_raw, Wk), (wv_raw, Wv), (wo_raw, Wo), (w1_s, W1), (w2_s, W2), (w3_s, W3)):
                sp.dma_start(dst[:], src.rearrange("(k p) n -> p k n", p=P)).then_inc(weights_landed, 16)
            for dst, src in ((bq_s, bq), (bk_s, bk), (bv_s, bv)):
                sp.dma_start(dst[:], src.rearrange("(k p) -> p k", p=P), allow_slow_non_contiguous=True).then_inc(weights_landed, 16)
            for dst, src in ((bo_raw, bo), (bf_raw, b_ffn)):
                sp.dma_start(dst[:], src.rearrange("(a n) -> a n", a=1)).then_inc(weights_landed, 16)
            for j, src in enumerate((g_xattn, g_ffn)):
                sp.dma_start(gates[:, j:j + 1], src.rearrange("(a n) -> a n", a=1).to_broadcast([P, 1])).then_inc(weights_landed, 16)
            sp.dma_start(mask_i[:], mask[0, 0]).then_inc(weights_landed, 16)

            def early(value, most):
                return value if isinstance(value, int) else sp.snap(value, min_val=0, max_val=most)

            def load_x(p):
                n = early(p.n, NP - 1)
                wait(sp, y_ready, p.times(1, -3))
                sp.dma_start(x_in[p.rem][:], x_v[:, bass.ds(n, 1)].rearrange("s p b e -> s (p b) e")).then_inc(x_landed[p.rem], 16)

            def load_ctx(p):
                n = early(p.n, NP - 1)
                wait(sp, cT_done, p.times(1, -1))
                sp.dma_start(ctx_in[p.rem % 2][:], ctx_v[:, bass.ds(n, 1)].rearrange("s p b e -> s (p b) e")).then_inc(ctx_landed[p.rem % 2], 16)

            def spread(p):
                sp.wait_ge(k_ready, p.times(1, 1))
                for h in range(HT):
                    rows = slice(h * D, (h + 1) * D)
                    sp.dma_start(k_blocks[p.rem % 2][rows, :, h, :].bitcast(F32),
                                 kT[rows, :, :, :].rearrange("d a m n -> d (a m) n").bitcast(F32)).then_inc(blocks_landed[p.rem % 2], 16)

            def store(p):
                n, written = early(p.n, NP - 1), early(p.times(1, 1), NP)
                sp.wait_ge(res_ready, written)
                sp.dma_start(out_v[:, bass.ds(n, 1)].rearrange("s p b e -> s (p b) e"), res[p.rem % 2][:]).then_inc(out_stored[p.rem % 2], 16)

            sp.wait_ge(setup_dve, BIAS_SPLIT)
            for i in range(2):
                sp.dma_start(bias_rows[i][1:2, :].bitcast(F32), bias_low[0:1, i, :].bitcast(F32)).then_inc(bias_landed, 16)

            def body(t):
                if t.known and t.n == 0:
                    load_ctx(t)
                    load_x(t)
                    load_x(t.back(-1))
                if t.back(-1).exists():
                    load_ctx(t.back(-1))
                if t.exists():
                    spread(t)
                if t.back(-2).exists():
                    load_x(t.back(-2))
                if t.back(2).exists():
                    store(t.back(2))

            turns(sp, body)
            for o in out_stored:
                sp.wait_ge(o, 16 * (NP // 2))

        @block.gpsimd
        def _(pool):
            nc.gpsimd.memset(ident[:], 0.0).then_inc(consts_ready, 1)
            nc.gpsimd.memset(ident_h[:], 0.0).then_inc(consts_ready, 1)
            for tile, value in ((c_zero, 0.0), (c_eps, EPS), (c_minus_half, -0.5), (c_three_halves, 1.5)):
                nc.gpsimd.memset(tile[:], value)
            nc.gpsimd.memset(ones_row[:], 1.0)
            nc.gpsimd.memset(ones_sq[:].bitcast(F32), 1.0)
            for i in range(2):
                nc.gpsimd.memset(bias_rows[i][:].bitcast(F32), 0.0).then_inc(consts_ready, 1)
            pool.wait_ge(consts_ready, 4)
            for m in (ident, ident_h):
                nc.gpsimd.affine_select(out=m[:], in_=m[:], compare_op=ALU.not_equal, fill=1.0, base=0,
                                        pattern=[[-1, P]], channel_multiplier=1).then_inc(consts_ready, 1)
            for i in range(2):
                nc.gpsimd.memset(k_blocks[i][:].rearrange("p a b c -> p (a b c)").bitcast(F32), 0.0).then_inc(consts_ready, 1)
                nc.gpsimd.memset(v_ones[i][:].rearrange("p a b c -> p (a b c)"), 1.0).then_inc(consts_ready, 1)

            def rstd(which, before):
                vp, r, a, b, nm = (ln_t[:, which, j, :] for j in range(5))
                mean, var = stat2[:, which, :, 0], stat2[:, which, :, 1]
                done = [0]

                def step(out, in0, in1, op):
                    nc.gpsimd.tensor_tensor(out, in0, in1, op).then_inc(pool_step, 1)
                    done[0] += 1
                    pool.wait_ge(pool_step, before + done[0])

                step(vp, var, c_eps[:], ALU.add)
                step(r, vp, c_minus_half[:], ALU.pow)
                for _ in range(NEWTON):
                    step(a, r, r, ALU.mult)
                    step(b, a, vp, ALU.mult)
                    step(a, b, c_minus_half[:], ALU.mult)
                    step(b, a, c_three_halves[:], ALU.add)
                    step(r, r, b, ALU.mult)
                step(a, mean, r, ALU.mult)
                step(nm, c_zero[:], a, ALU.subtract)
                pool.sem_inc(ln_constants, 1)
                assert done[0] == per_ln

            per_ln = 2 + 5 * NEWTON + 2

            def normalise(which, dst, src, ready):
                for b in range(PAIR):
                    last = nc.gpsimd.tensor_scalar(dst[:, b, :], src[:, b, :], ln_t[:, which, 1, b:b + 1],
                                                   ln_t[:, which, 4, b:b + 1], ALU.mult, ALU.add)
                    last.then_inc(ready, 1)

            STEPS_A, STEPS_C = per_ln, per_ln + 1

            def body(t):
                nxt, c = t.back(-1), t.back(2)
                if t.known:
                    before_1 = STEPS_A * min(t.n + (t.n > 0), NP) + STEPS_C * max(0, t.n - 2)
                    before_2 = STEPS_A * min(t.n + 2, NP) + STEPS_C * max(0, t.n - 2)
                else:
                    before_1 = t.times(STEPS_A + STEPS_C, STEPS_A - 2 * STEPS_C)
                    before_2 = t.times(STEPS_A + STEPS_C, 2 * STEPS_A - 2 * STEPS_C)

                def norm_1(p, before):
                    wait(pool, xT_done, p.times(1, 0))
                    pool.wait_ge(x_landed[p.rem], p.lap(BODY, 16))
                    pool.wait_ge(stat1_ready, p.times(1, 1))
                    rstd(0, before)
                    normalise(0, xn, x_in[p.rem], xn_ready)

                if t.known and t.n == 0:
                    norm_1(t, 0)
                    before_1 = STEPS_A
                if nxt.exists():
                    norm_1(nxt, before_1)
                if c.exists():
                    wait(pool, yT_done, c.times(1, 0))
                    pool.wait_ge(y_ready, c.times(1, 1))
                    pool.wait_ge(stat2_ready, c.times(1, 1))
                    rstd(1, before_2)
                    normalise(1, yn, y[c.rem % 2], yn_ready)
                    pool.wait_ge(th_ready, c.times(1, 1))
                    nc.gpsimd.tensor_tensor(tg[:], th[:].rearrange("p b e -> p (b e)"), tgates[:, 1:2].to_broadcast([P, PAIR * E]),
                                            ALU.mult).then_inc(pool_step, 1)
                    pool.wait_ge(pool_step, before_2 + STEPS_C)
                    wait(pool, out_stored[c.rem % 2], c.lap(2, 16) - 16)
                    nc.gpsimd.tensor_tensor(res[c.rem % 2][:].rearrange("p b e -> p (b e)"), tg[:],
                                            y[c.rem % 2][:].rearrange("p b e -> p (b e)"), ALU.add).then_inc(res_ready, 1)

            pool.wait_ge(setup_act, 1)
            turns(pool, body)

        @block.tensor
        def _(pe):
            read_by = {"u0": (attn_ready, PAIR, 1, 2), "u1": (attn_ready, PAIR, 2, 2), "xT": (xT_ready, 1, 1, 0),
                       "cT": (cT_ready, 1, 1, 0), "aT": (aT_ready, 1, 1, 2), "k": (k_ready, 1, 1, 0),
                       "o": (y_ready, 1, 1, 2), "q": (q_ready, 1, 1, 0), "v": (v_ready, 1, 1, 0),
                       "yT": (yT_ready, 1, 1, 2), "f": (th_ready, 1, 1, 2)}

            def bank_of(name, t):
                k, turn, bank = STEPS.index(name), t, BANK[name]
                while True:
                    k -= 1
                    if k < 0:
                        k, turn = len(STEPS) - 1, turn.back(1)
                    if turn.known and turn.n < 0:
                        return ps_m[bank]
                    semaphore, per, nth, lag = read_by[STEPS[k]]
                    if BANK[STEPS[k]] == bank and turn.back(lag).exists():
                        pe.wait_ge(semaphore, turn.back(lag).times(per, nth))
                        return ps_m[bank]

            def transposes(dst, src):
                for k in range(KT):
                    for b in range(PAIR):
                        last = nc.tensor.transpose(dst[:, k * TOK + b * P:k * TOK + (b + 1) * P], src[b][:, k * P:(k + 1) * P], ident[:])
                return last

            PARTS = ((0, 0), (0, 1), (1, 0))

            def project_T(dst, w, src):
                for m in range(KT):
                    terms = [(k, a, b) for k in range(KT) for a, b in PARTS]
                    for n, (k, a, b) in enumerate(terms):
                        last = nc.tensor.matmul(dst[:, m * TOK:(m + 1) * TOK], w[:, a, k, m * P:(m + 1) * P], src[:, b, k, :],
                                                start=(n == 0), stop=(n == len(terms) - 1))
                return last

            def project(dst, src, w, bias=None):
                for i in range(PAIR):
                    o = dst[:, i * E:(i + 1) * E]
                    if bias is not None:
                        nc.tensor.matmul(o, ones_sq[:], bias[:], start=True, stop=False)
                    terms = [(k, a, b) for k in range(KT) for a, b in PARTS]
                    for n, (k, a, b) in enumerate(terms):
                        last = nc.tensor.matmul(o, src[:, a, k, i * P:(i + 1) * P], w[:, b, k, :],
                                                start=(n == 0 and bias is None), stop=(n == len(terms) - 1))
                return last

            def setup():
                pe.wait_ge(weights_landed, 16 * 15)
                pe.wait_ge(consts_ready, 10)

                def transpose_w(w):
                    for k in range(KT):
                        for j in range(KT):
                            last = nc.tensor.transpose(ps_m[0][:, j * E + k * P:j * E + (k + 1) * P], w[:, k, j * P:(j + 1) * P], ident[:])
                    last.then_inc(setup_pe, 1)

                def product(rhs):
                    for m in range(KT):
                        for k in range(KT):
                            last = nc.tensor.matmul(ps_m[1][:, m * E:(m + 1) * E], wT_s[:, k, m * P:(m + 1) * P], rhs[:, k, :],
                                                    start=(k == 0), stop=(k == KT - 1))
                    last.then_inc(setup_pe, 1)

                transpose_w(w2_s)
                pe.wait_ge(setup_dve, 2)
                product(w3_s)
                pe.wait_ge(setup_dve, 3)
                transpose_w(w1_s)
                pe.wait_ge(setup_dve, 4)
                product(w23_s)
                pe.wait_ge(setup_dve, 5)
                o = ps_m[0][0:1, 0:E]
                nc.tensor.matmul(o, ones_row[0:1, 0:1], bo_raw[:], start=True, stop=False)
                for k in range(KT):
                    last = nc.tensor.matmul(o, bv_s[:, k:k + 1], wo_raw[:, k, :], start=False, stop=(k == KT - 1))
                last.then_inc(setup_pe, 1)
                pe.wait_ge(setup_dve, WEIGHTS_SPLIT)
                pe.wait_ge(bias_landed, 32)

            def scores(b, u):
                n, g = u // GROUPS, u % GROUPS
                m, h0 = g * G // HT, g * G % HT
                if u == 0:
                    pe.wait_ge(q_ready, b.times(1, 1))
                    pe.wait_ge(blocks_landed[b.rem % 2], b.lap(2, 16 * HT))
                wait(pe, shifted_ready, b.times(UNITS, u - 1))
                s = ps_s[u % 2]
                nc.tensor.matmul(s[:], ident_h[:], mask_bias[:], start=True, stop=False)
                for i, (a, c) in enumerate(PARTS):
                    last = nc.tensor.matmul(s[:], qT[b.rem % 2][:, a, m, n * P:(n + 1) * P],
                                            k_blocks[b.rem % 2][:, c * KT + m, h0:h0 + G, n * P:(n + 1) * P],
                                            start=False, stop=(i == len(PARTS) - 1))
                last.then_inc(s_done, 1)

            def transpose_probs(b, u):
                pe.wait_ge(probs_ready, b.times(UNITS, u + 1))
                wait(pe, pT_ready, b.times(UNITS, u - 1))
                for h in range(G):
                    last = nc.tensor.transpose(ps_pT[u % 2][:, h, :], probs[u % 2][:, h, :], ident[:])
                last.then_inc(pT_done, 1)

            def weigh_values(b, u):
                n, g = u // GROUPS, u % GROUPS
                if u == 0:
                    pe.wait_ge(v_ready, b.times(1, 1))
                if g == 0:
                    wait(pe, uT_ready, b.times(PAIR, n))
                pe.wait_ge(pT_ready, b.times(UNITS, u + 1))
                for h in range(G):
                    last = nc.tensor.matmul(ps_uT[h * SLOT:(h + 1) * SLOT, g, :], v_ones[b.rem % 2][:, n, g * G + h, :],
                                            pT[u % 2][:, h, :], start=True, stop=True, tile_position=(0, h * SLOT))
                last.then_inc(pv_done, 1)

            def untranspose(c, n):
                dst = bank_of(f"u{n}", c.back(-2))
                pe.wait_ge(uT_ready, c.times(PAIR, n + 1))
                for g in range(GROUPS):
                    last = nc.tensor.transpose(dst[:, g * P:(g + 1) * P], uT[n][:, g, :], ident[:])
                last.then_inc(u_done, 1)

            def body(t):
                b, c = t.back(1), t.back(2)
                A, B, C = t.exists(), b.exists(), c.exists()

                def attend(u):
                    if B:
                        transpose_probs(b, u)
                    if u > 0 and B:
                        weigh_values(b, u - 1)
                    if u == 0 and C:
                        weigh_values(c, UNITS - 1)

                def ahead(u):
                    if B and u < UNITS:
                        scores(b, u)

                def step(name, present, ready, count, work, done):
                    if present:
                        dst = bank_of(name, t)
                        if ready is not None:
                            pe.wait_ge(ready, count)
                        work(dst).then_inc(done, 1)

                def pair_of(tiles):
                    return lambda dst: transposes(dst, tiles)

                def plain(src):
                    return [src[:, i, :] for i in range(PAIR)]

                ahead(1)
                if C:
                    untranspose(c, 0)
                step("xT", A, xn_ready, t.times(PAIR, PAIR), pair_of(plain(xn)), xT_done)
                attend(0)
                ahead(2)
                if C:
                    untranspose(c, 1)
                step("cT", A, ctx_landed[t.rem % 2], t.lap(2, 16), pair_of(plain(ctx_in[t.rem % 2])), cT_done)
                attend(1)
                ahead(3)
                step("aT", C, attn_ready, c.times(PAIR, PAIR), pair_of([a[:].rearrange("p h d -> p (h d)") for a in attn]), aT_done)
                attend(2)
                ahead(4)
                step("k", A, cT_ready, t.times(1, 1), lambda dst: project_T(dst, wk_s, cT), k_done)
                attend(3)
                ahead(5)
                step("o", C, aT_ready, c.times(1, 1), lambda dst: project(dst, aT, wo_s, bias_rows[0]), o_done)
                attend(4)
                ahead(6)
                step("q", A, xT_ready, t.times(1, 1), lambda dst: project_T(dst, wq_s, xT), q_done)
                attend(5)
                ahead(7)
                step("v", A, cT_ready, t.times(1, 1), lambda dst: project(dst, cT, wv_s), v_done)
                step("yT", C, yn_ready, c.times(PAIR, PAIR), pair_of(plain(yn)), yT_done)
                attend(6)
                if A:
                    scores(t, 0)
                step("f", C, yT_ready, c.times(1, 1), lambda dst: project(dst, yT, wf_s, bias_rows[1]), f_done)
                attend(7)

            setup()
            turns(pe, body)

        @block.scalar
        def _(act):
            act.wait_ge(weights_landed, 16 * 15)
            nc.scalar.activation(tgates[:], gates[:], ACT.Tanh).then_inc(setup_act, 1)

            def flat(a):
                return a[:].rearrange("p a b -> p (a b)")

            def copy(dst, src, ready):
                nc.scalar.activation(dst, src, ACT.Copy).then_inc(ready, 1)

            def high(dst, name, done, count, free, freed, ready, bias=None):
                act.wait_ge(done, count)
                wait(act, free, freed)
                src = ps_m[BANK[name]]
                if bias is None:
                    last = nc.scalar.activation(dst[:, 0].rearrange("p k n -> p (k n)"), src[:], ACT.Copy)
                else:
                    for m in range(KT):
                        last = nc.scalar.activation(dst[:, 0, m, :], src[:, m * TOK:(m + 1) * TOK], ACT.Identity, bias=bias[:, m:m + 1])
                last.then_inc(ready, 1)

            def expo(b, u):
                act.wait_ge(shifted_ready, b.times(UNITS, u + 1))
                wait(act, pT_done, b.times(UNITS, u - 1))
                nc.scalar.activation(flat(probs[u % 2]), flat(shifted[u % 2]), ACT.Exp,
                                     scale=float(D) ** -0.5).then_inc(probs_ready, 1)

            def copy_pT(b, u):
                act.wait_ge(pT_done, b.times(UNITS, u + 1))
                wait(act, pv_done, b.times(UNITS, u - 1))
                copy(flat(pT[u % 2]), flat(ps_pT[u % 2]), pT_ready)

            def copy_uT(b, n):
                act.wait_ge(pv_done, b.times(UNITS, (n + 1) * GROUPS))
                wait(act, u_done, b.times(PAIR, n - 1))
                copy(flat(uT[n]), flat(ps_uT), uT_ready)

            def body(t):
                b, c = t.back(1), t.back(2)
                A, B, C = t.exists(), b.exists(), c.exists()

                def attend(u):
                    if u == 0 and C:
                        copy_pT(c, UNITS - 1)
                    if u > 0 and B:
                        copy_pT(b, u - 1)
                    if B:
                        expo(b, u)

                attend(0)
                if A:
                    high(xT, "xT", xT_done, t.times(1, 1), q_done, t.times(1, 0), xT_high)
                attend(1)
                if C:
                    copy_uT(c, 1)
                if A:
                    high(cT, "cT", cT_done, t.times(1, 1), v_done, t.times(1, 0), cT_high)
                attend(2)
                if C:
                    high(aT, "aT", aT_done, c.times(1, 1), o_done, c.times(1, 0), aT_high)
                attend(3)
                if A:
                    wait(act, s_done, t.times(UNITS, -UNITS))
                    if not t.known or t.n > 0:
                        act.wait_ge(blocks_landed[(t.rem - 1) % 2], t.back(1).lap(2, 16 * HT))
                    high(kT, "k", k_done, t.times(1, 1), cT_ready, t.times(1, 0), k_high, bk_s)
                attend(4)
                attend(5)
                if B:
                    copy_uT(b, 0)
                if A:
                    high(qT[t.rem % 2], "q", q_done, t.times(1, 1), xT_ready, t.times(1, 0), q_high, bq_s)
                attend(6)
                if A:
                    act.wait_ge(v_done, t.times(1, 1))
                    wait(act, pv_done, t.times(UNITS, -UNITS))
                    nc.scalar.activation(v_ones[t.rem % 2][:, :, :, 0:D],
                                         ps_m[BANK["v"]][:].rearrange("p (b h d) -> p b h d", b=PAIR, d=D), ACT.Copy).then_inc(v_ready, 1)
                if C:
                    high(yT, "yT", yT_done, c.times(1, 1), f_done, c.times(1, 0), yT_high)
                attend(7)
                if C:
                    act.wait_ge(f_done, c.times(1, 1))
                    wait(act, res_ready, c.times(1, 0))
                    nc.scalar.activation(flat(th), ps_m[BANK["f"]][:], ACT.Tanh).then_inc(th_ready, 1)

            turns(act, body)

        @block.vector
        def _(dve):
            dve.wait_ge(weights_landed, 16 * 15)
            for h in range(G):
                last = nc.vector.tensor_scalar(mask_bias[:, h, :], mask_i[:], 0, MASKED, ALU.is_equal, ALU.mult)
            last.then_inc(setup_dve, 1)
            def flat(a):
                return a.rearrange("p k n -> p (k n)")

            for n, (dst, bank) in enumerate(((wT_s, 0), (w23_s, 1), (wT_s, 0), (w123_s, 1))):
                dve.wait_ge(setup_pe, n + 1)
                nc.vector.tensor_copy(flat(dst[:]), ps_m[bank][:]).then_inc(setup_dve, 1)
            dve.wait_ge(setup_pe, 5)
            dve.wait_ge(setup_act, 1)
            nc.vector.tensor_scalar(bo_g[:], ps_m[0][0:1, 0:E], tgates[0:1, 0:1], None, ALU.mult).then_inc(setup_dve, 1)
            nc.vector.tensor_scalar(flat(wo_g[:]), flat(wo_raw[:]), tgates[:, 0:1], None, ALU.mult).then_inc(setup_dve, 1)
            dve.wait_ge(consts_ready, 10)
            dve.wait_ge(setup_dve, 7)
            biases = ((bias_rows[0], bo_g, 0), (bias_rows[1], bf_raw, 1))
            weights = ((wq_s, wq_raw), (wk_s, wk_raw), (wv_s, wv_raw), (wo_s, wo_g), (wf_s, w123_s))
            for rows, src, i in biases:
                last = nc.vector.tensor_copy(rows[0:1, :], src[:])
            for dst, src in weights:
                last = nc.vector.tensor_copy(flat(dst[:, 0]), flat(src[:]))
            last.then_inc(setup_dve, 1)
            dve.wait_ge(setup_dve, 8)
            for rows, src, i in biases:
                last = nc.vector.tensor_tensor(bias_low[:, i, :], src[:], rows[0:1, :], ALU.subtract)
            last.then_inc(setup_dve, 1)
            for dst, src in weights:
                last = nc.vector.tensor_tensor(flat(dst[:, 1]), flat(src[:]), flat(dst[:, 0]), ALU.subtract)
            last.then_inc(setup_dve, 1)

            STEPS_A, STEPS_B, STEPS_C = 1, UNITS, 1 + PAIR

            def body(t):
                nxt, b, c = t.back(-1), t.back(1), t.back(2)
                A, B, C = t.exists(), b.exists(), c.exists()
                done = [0]
                if t.known:
                    before = STEPS_A * min(t.n + (t.n > 0), NP) + STEPS_B * max(0, t.n - 1) + STEPS_C * max(0, t.n - 2)
                else:
                    before = t.times(STEPS_A + STEPS_B + STEPS_C, STEPS_A - STEPS_B - 2 * STEPS_C)

                def step(inst):
                    inst.then_inc(dve_step, 1)
                    done[0] += 1
                    dve.wait_ge(dve_step, before + done[0])


                def soften(u, stats=None):
                    if stats is not None:
                        which, src, ready = stats
                        for i in range(PAIR):
                            last = nc.vector.bn_stats(stat6[:, which, i, :], src[:, i, :])
                        last.then_inc(dve_step, 1)
                        done[0] += 1
                        if not B:
                            dve.wait_ge(dve_step, before + done[0])
                    if B:
                        maximum(u)
                    if stats is not None:
                        for i in range(PAIR):
                            last = nc.vector.bn_aggr(stat2[:, which, i, :], stat6[:, which, i, :])
                        last.then_inc(ready, 1)

                def maximum(u):
                    dve.wait_ge(s_done, b.times(UNITS, u + 1))
                    step(nc.vector.tensor_reduce(row_max[u % 2][:], ps_s[u % 2][:], axis=AX.X, op=ALU.max))
                    wait(dve, probs_ready, b.times(UNITS, u - 1))
                    nc.vector.tensor_tensor(shifted[u % 2][:], ps_s[u % 2][:], row_max[u % 2][:].unsqueeze(2).to_broadcast([P, G, P]),
                                            ALU.subtract).then_inc(shifted_ready, 1)

                def normalise(n):
                    if not C:
                        return
                    dve.wait_ge(u_done, c.times(PAIR, n + 1))
                    u = ps_m[BANK[f"u{n}"]][:].rearrange("p (h s) -> p h s", s=SLOT)
                    step(nc.vector.reciprocal(den_r[n][:], u[:, :, D]))
                    wait(dve, aT_done, c.times(1, 0))
                    nc.vector.tensor_tensor(attn[n][:], u[:, :, 0:D], den_r[n][:].unsqueeze(2).to_broadcast([P, H, D]),
                                            ALU.mult).then_inc(attn_ready, 1)

                def low(dst, name, high_ready, count, ready, bias=None):
                    dve.wait_ge(high_ready, count)
                    src = ps_m[BANK[name]]
                    if bias is None:
                        last = nc.vector.tensor_tensor(flat(dst[:, 1]), src[:], flat(dst[:, 0]), ALU.subtract)
                    else:
                        for m in range(KT):
                            last = nc.vector.scalar_tensor_tensor(dst[:, 1, m, :], src[:, m * TOK:(m + 1) * TOK], bias[:, m:m + 1],
                                                                  dst[:, 0, m, :], ALU.add, ALU.subtract)
                    last.then_inc(ready, 1)

                def stats_of_x(p):
                    dve.wait_ge(x_landed[p.rem], p.lap(BODY, 16))
                    wait(dve, xn_ready, p.times(PAIR, 0))
                    return 0, x_in[p.rem], stat1_ready

                def stats_of_y():
                    wait(dve, yn_ready, c.times(PAIR, 0))
                    dve.wait_ge(y_ready, c.times(1, 1))
                    return 1, y[c.rem % 2], stat2_ready

                if t.known and t.n == 0:
                    soften(0, stats_of_x(t))
                for u in range(UNITS):
                    stats = None
                    if u == 2 and nxt.exists():
                        stats = stats_of_x(nxt)
                    if u == 6 and C:
                        stats = stats_of_y()
                    soften(u, stats)
                    if u in (1, 2):
                        normalise(u - 1)
                    if u == 1 and A:
                        low(xT, "xT", xT_high, t.times(1, 1), xT_ready)
                    if u == 2 and A:
                        low(cT, "cT", cT_high, t.times(1, 1), cT_ready)
                    if u == 3 and C:
                        low(aT, "aT", aT_high, c.times(1, 1), aT_ready)
                    if u == 4 and A:
                        low(kT, "k", k_high, t.times(1, 1), k_ready, bk_s)
                    if u == 5 and C:
                        dve.wait_ge(o_done, c.times(1, 1))
                        wait(dve, res_ready, c.times(1, -1))
                        nc.vector.tensor_tensor(flat(y[c.rem % 2][:]), ps_m[BANK["o"]][:], flat(x_in[c.rem][:]),
                                                ALU.add).then_inc(y_ready, 1)
                    if u == 6 and A:
                        low(qT[t.rem % 2], "q", q_high, t.times(1, 1), q_ready, bq_s)
                if C:
                    low(yT, "yT", yT_high, c.times(1, 1), yT_ready)

            turns(dve, body)


_INS = ["x", "ctx_1024", "mask_1x1xSxS2_ik0", "g_xattn", "g_ffn", "L0_xattn_Wv", "L0_xattn_bv", "L0_xattn_Wk",
        "L0_xattn_bk", "L0_xattn_Wq", "L0_xattn_bq", "L0_xattn_Wo", "L0_xattn_bo", "L0_ffn_weight",
        "L0_ffn_aux_weight1", "L0_ffn_aux_weight2", "L0_ffn_bias"]


def kernel(**inputs):
    import numpy as np
    import concourse.bacc as bacc
    from concourse.bass_utils import run_bass_kernel_spmd

    nc = bacc.Bacc("TRN2", target_bir_lowering=False, num_devices=1)
    arrays, args = {}, []
    for name in _INS:
        a = np.ascontiguousarray(inputs[name])
        arrays[f"in_{name}"] = a
        args.append(nc.dram_tensor(f"in_{name}", a.shape, mybir.dt.from_np(a.dtype), kind="ExternalInput").ap())
    shape = np.shape(inputs["x"])
    args.append(nc.dram_tensor("out_0", shape, F32, kind="ExternalOutput").ap())
    gated_xattn_block(nc, *args)
    r = run_bass_kernel_spmd(nc, [arrays], core_ids=[0])
    return r.results[0]["out_0"]
```

```python
from contextlib import ExitStack

import concourse.bass as bass
from concourse import mybir

F32 = mybir.dt.float32
F32R = mybir.dt.float32r
I32 = mybir.dt.int32
ACT = mybir.ActivationFunctionType
ALU = mybir.AluOpType
AX = mybir.AxisListType

P = 128
E = 256
KT = E // P
H = 16
D = E // H
HT = P // D
G = 4
HALF = P // 2
GROUPS = H // G
PAIR = 2
TOK = PAIR * P
UNITS = PAIR * GROUPS
SLOT = 2 * D
EPS = 1e-5
FAR = 2.0 ** 100


def gated_xattn_block(nc, x, ctx, mask, g_xattn, g_ffn, Wv, bv, Wk, bk, Wq, bq, Wo, bo,
                      W1, W2, W3, b_ffn, out):
    N = x.shape[0]
    NP = N // PAIR
    BODY = 4

    x_v = x.rearrange("(p b) s e -> s p b e", b=PAIR)
    ctx_v = ctx.rearrange("(p b) s e -> s p b e", b=PAIR)
    out_v = out.rearrange("(p b) s e -> s p b e", b=PAIR)

    with ExitStack() as stack:
        def sb(name, shape, dt=F32):
            return stack.enter_context(nc.sbuf_tensor(name, shape, dt))

        def psum(name, shape):
            return stack.enter_context(nc.psum_tensor(name, shape, F32))

        def sem(name):
            return stack.enter_context(nc.semaphore(name))

        ident = sb("ident", [P, P])
        mask_i = sb("mask_i", [P, P], I32)
        far = sb("far", [P, P])
        wq_raw, wk_raw, wv_raw = (sb(n, [P, KT, E]) for n in ("wq_raw", "wk_raw", "wv_raw"))
        wq_s, wk_s, wv_s, wo_s, wf_s = (sb(n, [P, 2, KT, E], F32R) for n in ("wq_s", "wk_s", "wv_s", "wo_s", "wf_s"))
        wo_raw, w1_s, w2_s, w3_s = (sb(n, [P, KT, E]) for n in ("wo_raw", "w1_s", "w2_s", "w3_s"))
        wq_neg, wk_sorted = sb("wq_neg", [P, KT, E]), sb("wk_sorted", [P, KT, E])
        bqk_raw, bqk_sorted = sb("bqk_raw", [1, 2, E]), sb("bqk_sorted", [1, 2, E])
        bqk_low = sb("bqk_low", [1, 2, E], F32R)
        bqk_rows = sb("bqk_rows", [P, 2, E], F32R)
        bv_s = sb("bv_s", [P, KT])
        bo_raw = sb("bo_raw", [1, E])
        bv_wide = sb("bv_wide", [P, KT, P])
        bo_g = sb("bo_g", [P, E])
        bf_raw = sb("bf_raw", [1, E])
        bf_low = sb("bf_low", [1, E], F32R)
        bf_rows = sb("bf_rows", [P, E], F32R)
        ones_wide = sb("ones_wide", [P, TOK], F32R)
        c_zero, c_eps, c_minus_half, c_three_halves = (sb(n, [P, 2 * PAIR]) for n in (
            "c_zero", "c_eps", "c_minus_half", "c_three_halves"))
        ones_row = sb("ones_row", [1, P])
        gates = sb("gates", [P, 2])
        tgates = sb("tgates", [P, 2])

        x_in = [sb(f"x_in{i}", [P, PAIR, E]) for i in range(BODY)]
        ctx_in = [sb(f"ctx_in{i}", [P, PAIR, E]) for i in range(2)]
        xn = sb("xn", [P, PAIR, E])
        xT = sb("xT", [P, 2, KT, TOK], F32R)
        cT = sb("cT", [P, 2, KT, TOK], F32R)
        qT = sb("qT", [P, 2, KT, TOK], F32R)
        kT = sb("kT", [P, 2, KT, TOK], F32R)
        q_parts = [sb(f"q_parts{i}", [P, 2, KT, TOK], F32R) for i in range(2)]
        k_blocks = [sb(f"k_blocks{i}", [P, 2 * KT, HT, TOK], F32R) for i in range(2)]
        v_gap = [sb(f"v_gap{i}", [P, PAIR, H // 2, 3, D]) for i in range(2)]
        y = [sb(f"y{i}", [P, PAIR, E]) for i in range(BODY)]
        yn = sb("yn", [P, PAIR, E])
        yT = sb("yT", [P, 2, KT, TOK], F32R)
        th = sb("th", [P, PAIR, E])
        th_gated = sb("th_gated", [P, PAIR, E])
        stat6 = sb("stat6", [P, 2, PAIR, 6])
        stat2 = sb("stat2", [P, 2, PAIR, 2])
        ln_t = sb("ln_t", [P, 5, 2 * PAIR])

        wo_g, wT_s, w23_s, w123_s = th_gated, y[1], y[2], y[3]

        negs = [sb(f"negs{i}", [P, G, P]) for i in range(2)]
        neg_max = [sb(f"neg_max{i}", [P, G]) for i in range(2)]
        probs = [sb(f"probs{i}", [P, G, P]) for i in range(4)]
        den = [sb(f"den{i}", [P, G]) for i in range(4)]
        den_r = [sb(f"den_r{i}", [P, G]) for i in range(4)]
        att = [sb(f"att{i}", [P, G, P]) for i in range(2)]
        attT = [sb(f"attT{i}", [P, G, P]) for i in range(2)]
        aT = sb("aT", [P, 2, KT, TOK], F32R)

        ps_s = [psum(f"ps_s{i}", [P, G, P]) for i in range(2)]
        ps_attT = [psum(f"ps_attT{i}", [P, G, P]) for i in range(2)]
        ps_a = psum("ps_a", [P, KT, TOK])
        ps_m = [psum(f"ps_m{i}", [P, 512]) for i in range(3)]
        STEPS = ("v", "cT", "q", "o", "k", "yT", "f", "xT")
        BANK = {name: i % len(ps_m) for i, name in enumerate(STEPS)}

        first_landed = sem("first_landed")
        later_landed = sem("later_landed")
        consts_ready = sem("consts_ready")
        setup_pe = sem("setup_pe")
        setup_act = sem("setup_act")
        setup_dve = sem("setup_dve")
        x_landed = [sem(f"x_landed{i}") for i in range(BODY)]
        ctx_landed = [sem(f"ctx_landed{i}") for i in range(2)]
        q_landed = [sem(f"q_landed{i}") for i in range(2)]
        blocks_landed = [sem(f"blocks_landed{i}") for i in range(2)]
        y_free = [sem(f"y_free{i}") for i in range(BODY)]
        (stat1_ready, xn_ready, xT_done, xT_high, xT_ready, cT_done, cT_high, cT_ready, k_done,
         k_high, k_ready, q_done, q_high, q_ready, v_done, v_ready, s_done, negs_ready, probs_ready,
         den_ready, att_ready, attT_done, attT_by_act, attT_by_dve, pv_done, aT_high, aT_ready,
         o_done, y_ready, stat2_ready, yn_ready, yT_done, yT_high, yT_ready, f_done, th_ready,
         res_ready, dve_step, pool_step, scores_seen, x_biased, gated, bias_landed) = (sem(n) for n in (
             "stat1_ready", "xn_ready", "xT_done", "xT_high", "xT_ready", "cT_done", "cT_high",
             "cT_ready", "k_done", "k_high", "k_ready", "q_done", "q_high", "q_ready", "v_done",
             "v_ready", "s_done", "negs_ready", "probs_ready", "den_ready", "att_ready",
             "attT_done", "attT_by_act", "attT_by_dve", "pv_done", "aT_high", "aT_ready", "o_done",
             "y_ready", "stat2_ready", "yn_ready", "yT_done", "yT_high", "yT_ready", "f_done",
             "th_ready", "res_ready", "dve_step", "pool_step", "scores_seen", "x_biased", "gated", "bias_landed"))

        CONSTS = 7
        FIRST, LATER = 16 * 9, 16 * 6
        (SORTED, SETUP_HIGH, BQK_LOW, SETUP_LOW, SETUP_Q, W2_T, W23, W1_T, W123, OUT_BIAS, LATER_HIGH, BF_LOW,
         LATER_LOW) = range(1, 14)

        block = stack.enter_context(nc.Block())

        class Pair:
            def __init__(self, quot, rem):
                self.quot, self.rem = quot + rem // BODY if rem // BODY else quot, rem % BODY
                self.n = self.quot * BODY + self.rem if self.rem else self.quot * BODY
                self.known = isinstance(self.n, int)

            def times(self, per, plus):
                return self.quot * (BODY * per) + (self.rem * per + plus)

            def lap(self, ring, per):
                return self.quot * (BODY // ring * per) + (self.rem // ring + 1) * per

            def back(self, k):
                return Pair(self.quot, self.rem - k)

            def exists(self):
                return not self.known or 0 <= self.n < NP

        def turns(eng, body):
            for t in range(BODY):
                body(Pair(0, t))
            with eng.Fori(1, NP // BODY - 1) as i:
                for r in range(BODY):
                    body(Pair(i, r))
            for t in range(NP - BODY, NP + 4):
                body(Pair(t // BODY, t % BODY))

        def wait(eng, semaphore, value):
            if not isinstance(value, int) or value > 0:
                eng.wait_ge(semaphore, value)

        def unit(b, u):
            return b.back(-(u // UNITS)), u % UNITS

        BY_ACT = (2, 5)
        BY_DVE = tuple(u for u in range(UNITS) if u not in BY_ACT)

        def copied(b, u):
            for semaphore, units in ((attT_by_act, BY_ACT), (attT_by_dve, BY_DVE)):
                if u in units:
                    return semaphore, b.times(len(units), units.index(u) + 1)

        @block.sync
        def _(sp):
            def load_weight(dst, src, landed):
                sp.dma_start(dst[:], src.rearrange("(k p) n -> p k n", p=P)).then_inc(landed, 16)

            def load_first():
                for dst, src in ((wk_raw, Wk), (wv_raw, Wv), (wq_raw, Wq)):
                    load_weight(dst, src, first_landed)
                for i, src in enumerate((bq, bk)):
                    sp.dma_start(bqk_raw[:, i, :], src.rearrange("(a n) -> a n", a=1)).then_inc(first_landed, 16)
                sp.dma_start(bv_s[:], bv.rearrange("(k p) -> p k", p=P), allow_slow_non_contiguous=True).then_inc(first_landed, 16)
                for j, src in enumerate((g_xattn, g_ffn)):
                    sp.dma_start(gates[:, j:j + 1], src.rearrange("(a n) -> a n", a=1).to_broadcast([P, 1])).then_inc(first_landed, 16)
                sp.dma_start(mask_i[:], mask[0, 0]).then_inc(first_landed, 16)

            def load_later():
                for dst, src in ((w2_s, W2), (w3_s, W3), (w1_s, W1), (wo_raw, Wo)):
                    load_weight(dst, src, later_landed)
                for dst, src in ((bo_raw, bo), (bf_raw, b_ffn)):
                    sp.dma_start(dst[:], src.rearrange("(a n) -> a n", a=1)).then_inc(later_landed, 16)

            def early(value, most):
                return value if isinstance(value, int) else sp.snap(value, min_val=0, max_val=most)

            def load_x(p):
                n = early(p.n, NP - 1)
                wait(sp, y_ready, p.times(1, -3))
                sp.dma_start(x_in[p.rem][:], x_v[:, bass.ds(n, 1)].rearrange("s p b e -> s (p b) e")).then_inc(x_landed[p.rem], 16)

            def load_ctx(p):
                n = early(p.n, NP - 1)
                wait(sp, cT_done, p.times(1, -1))
                sp.dma_start(ctx_in[p.rem % 2][:], ctx_v[:, bass.ds(n, 1)].rearrange("s p b e -> s (p b) e")).then_inc(ctx_landed[p.rem % 2], 16)

            def spread(p):
                sp.wait_ge(k_ready, p.times(1, 1))
                for h in range(HT):
                    rows = slice(h * D, (h + 1) * D)
                    sp.dma_start(k_blocks[p.rem % 2][rows, :, h, :].bitcast(F32),
                                 kT[rows, :, :, :].rearrange("d a m n -> d (a m) n").bitcast(F32)).then_inc(blocks_landed[p.rem % 2], 16)
                for h in range(HT):
                    rows, other = slice(h * D, (h + 1) * D), (h + HT // 2) % HT * D
                    sp.dma_start(k_blocks[p.rem % 2][other:other + D, 0:KT, h, :].bitcast(F32),
                                 kT[rows, 0, :, :].bitcast(F32)).then_inc(blocks_landed[p.rem % 2], 16)

            def spread_q(p):
                sp.wait_ge(q_ready, p.times(1, 1))
                for odd in range(2):
                    own, other = slice(odd * HALF, (odd + 1) * HALF), slice((1 - odd) * HALF, (2 - odd) * HALF)
                    for part, rows in ((0, own), (1, other)):
                        sp.dma_start(q_parts[p.rem % 2][rows, odd, :, :].bitcast(F32),
                                     qT[own, part, :, :].bitcast(F32)).then_inc(q_landed[p.rem % 2], 16)

            def store(p):
                n, written = early(p.n, NP - 1), early(p.times(1, 1), NP)
                sp.wait_ge(res_ready, written)
                sp.dma_start(out_v[:, bass.ds(n, 1)].rearrange("s p b e -> s (p b) e"), y[p.rem][:]).then_inc(y_free[p.rem], 16)

            def body(t):
                if t.known and t.n == 0:
                    load_ctx(t)
                    load_x(t)
                    load_first()
                    load_ctx(t.back(-1))
                    load_x(t.back(-1))
                    load_later()
                    sp.wait_ge(setup_dve, BQK_LOW)
                    sp.dma_start(bqk_rows[1:2, :, :].bitcast(F32), bqk_low[:].bitcast(F32)).then_inc(bias_landed, 16)
                    sp.wait_ge(consts_ready, CONSTS)
                    spread(t)
                if t.known and t.n == 1:
                    sp.wait_ge(setup_dve, BF_LOW)
                    sp.dma_start(bf_rows[1:2, :].bitcast(F32), bf_low[:].bitcast(F32)).then_inc(bias_landed, 16)
                if t.back(-2).exists():
                    load_ctx(t.back(-2))
                if t.exists():
                    spread_q(t)
                if t.back(-2).exists():
                    load_x(t.back(-2))
                if t.back(-1).exists():
                    spread(t.back(-1))
                if t.back(4).exists():
                    store(t.back(4))

            turns(sp, body)
            for free in y_free:
                sp.wait_ge(free, 16 * (NP // BODY + 1))

        @block.gpsimd
        def _(pool):
            nc.gpsimd.memset(ident[:], 0.0).then_inc(consts_ready, 1)
            for tile, value in ((c_zero, 0.0), (c_eps, EPS), (c_minus_half, -0.5), (c_three_halves, 1.5)):
                nc.gpsimd.memset(tile[:], value)
            nc.gpsimd.memset(ones_row[:], 1.0)
            for free in y_free:
                pool.sem_inc(free, 16)
            nc.gpsimd.memset(ones_wide[:].bitcast(F32), 1.0)
            nc.gpsimd.memset(bqk_rows[:].rearrange("p a b -> p (a b)").bitcast(F32), 0.0)
            nc.gpsimd.memset(bf_rows[:].bitcast(F32), 0.0).then_inc(consts_ready, 1)
            pool.wait_ge(consts_ready, 2)
            nc.gpsimd.affine_select(out=ident[:], in_=ident[:], compare_op=ALU.not_equal, fill=1.0, base=0,
                                    pattern=[[-1, P]], channel_multiplier=1).then_inc(consts_ready, 1)
            for i in range(2):
                nc.gpsimd.memset(v_gap[i][:].rearrange("p a b c d -> p (a b c d)"), 0.0).then_inc(consts_ready, 1)
            for i in range(2):
                nc.gpsimd.memset(k_blocks[i][:].rearrange("p a b c -> p (a b c)").bitcast(F32), 0.0).then_inc(consts_ready, 1)

            def rstd_steps(before, first, last):
                vp, r, a, b, nm = (ln_t[:, j, :] for j in range(5))
                moments = stat2[:].rearrange("p a b z -> p (a b) z")
                mean, var = moments[:, :, 0], moments[:, :, 1]
                steps = ((vp, var, c_eps[:], ALU.add), (r, vp, c_minus_half[:], ALU.pow),
                         (a, r, r, ALU.mult), (b, a, vp, ALU.mult), (a, b, c_minus_half[:], ALU.mult),
                         (b, a, c_three_halves[:], ALU.add), (r, r, b, ALU.mult),
                         (a, mean, r, ALU.mult), (nm, c_zero[:], a, ALU.subtract))
                assert len(steps) == RSTD
                for i in range(first, last):
                    nc.gpsimd.tensor_tensor(*steps[i]).then_inc(pool_step, 1)
                    pool.wait_ge(pool_step, before + i + 1)

            def normalise(which, dst, src, ready, i):
                j = which * PAIR + i
                nc.gpsimd.tensor_scalar(dst[:, i, :], src[:, i, :], ln_t[:, 1, j:j + 1], ln_t[:, 4, j:j + 1],
                                        ALU.mult, ALU.add).then_inc(ready, 1)

            RSTD = 9

            def weigh(b, u):
                pool.wait_ge(den_ready, b.times(UNITS, u + 1))
                wait(pool, attT_done, b.times(UNITS, u - 1))
                nc.gpsimd.tensor_tensor(att[u % 2][:], probs[u % 4][:], den_r[u % 4][:].unsqueeze(2).to_broadcast([P, G, P]),
                                        ALU.mult).then_inc(att_ready, 1)

            def body(t):
                nxt, b, d, e = t.back(-1), t.back(1), t.back(3), t.back(4)
                before = t.times(RSTD, RSTD)
                if t.known and t.n == 0:
                    pool.wait_ge(x_landed[0], 16)
                    pool.wait_ge(stat1_ready, 1)
                    rstd_steps(0, 0, RSTD)
                    for i in range(PAIR):
                        normalise(0, xn, x_in[0], xn_ready, i)
                for u in range(UNITS):
                    if unit(b, u + 1)[0].exists():
                        weigh(*unit(b, u + 1))
                    if u == 0 and (nxt.exists() or d.exists()):
                        if nxt.exists():
                            wait(pool, xT_done, nxt.times(1, 0))
                            pool.wait_ge(x_landed[nxt.rem], nxt.lap(BODY, 16))
                            pool.wait_ge(stat1_ready, nxt.times(1, 1))
                        if d.exists():
                            wait(pool, yT_done, d.times(1, 0))
                            pool.wait_ge(y_ready, d.times(1, 1))
                            pool.wait_ge(stat2_ready, d.times(1, 1))
                        rstd_steps(before, 0, 5)
                    if u == 1 and (nxt.exists() or d.exists()):
                        rstd_steps(before, 5, RSTD)
                    for i in range(PAIR):
                        if u == 2 and d.exists():
                            normalise(1, yn, y[d.rem], yn_ready, i)
                        if u == 3 and nxt.exists():
                            normalise(0, xn, x_in[nxt.rem], xn_ready, i)
                    if u == 4 and e.exists():
                        if e.known:
                            wait(pool, res_ready, e.times(1, 0))
                        pool.wait_ge(th_ready, e.times(1, 1))
                        nc.gpsimd.tensor_tensor(th_gated[:].rearrange("p b e -> p (b e)"), th[:].rearrange("p b e -> p (b e)"),
                                                tgates[:, 1:2].to_broadcast([P, PAIR * E]), ALU.mult).then_inc(gated, 1)
                    if u == 5 and b.exists():
                        if b.known and b.n == 0:
                            pool.wait_ge(setup_dve, OUT_BIAS)
                        nc.gpsimd.tensor_tensor(x_in[b.rem][:], x_in[b.rem][:], bo_g[:].unsqueeze(1).to_broadcast([P, PAIR, E]),
                                                ALU.add).then_inc(x_biased, 1)
                    if u == 6 and e.exists():
                        pool.wait_ge(gated, e.times(1, 1))
                        nc.gpsimd.tensor_tensor(y[e.rem][:].rearrange("p b e -> p (b e)"), th_gated[:].rearrange("p b e -> p (b e)"),
                                                y[e.rem][:].rearrange("p b e -> p (b e)"), ALU.add).then_inc(res_ready, 1)

            turns(pool, body)

        @block.tensor
        def _(pe):
            read_by = {"xT": (xT_ready, -1), "v": (v_ready, 0), "q": (q_ready, 0), "o": (y_ready, 2), "f": (th_ready, 3),
                       "cT": (cT_ready, -1), "yT": (yT_ready, 3), "k": (k_ready, -1)}

            def bank_of(name, t):
                k, turn, bank = STEPS.index(name), t, BANK[name]
                while True:
                    k -= 1
                    if k < 0:
                        k, turn = len(STEPS) - 1, turn.back(1)
                    if turn.known and turn.n < -1:
                        return ps_m[bank]
                    semaphore, lag = read_by[STEPS[k]]
                    if BANK[STEPS[k]] == bank and turn.back(lag).exists():
                        pe.wait_ge(semaphore, turn.back(lag).times(1, 1))
                        return ps_m[bank]

            def transposes(dst, src):
                for k in range(KT):
                    for b in range(PAIR):
                        last = nc.tensor.transpose(dst[:, k * TOK + b * P:k * TOK + (b + 1) * P], src[b][:, k * P:(k + 1) * P], ident[:])
                return last

            PARTS = ((0, 0), (0, 1), (1, 0))

            def project_T(dst, w, src, bias):
                for m in range(KT):
                    nc.tensor.matmul(dst[:, m * TOK:(m + 1) * TOK], bias[:, m * P:(m + 1) * P], ones_wide[:], start=True, stop=False)
                    terms = [(k, a, b) for k in range(KT) for a, b in PARTS]
                    for n, (k, a, b) in enumerate(terms):
                        last = nc.tensor.matmul(dst[:, m * TOK:(m + 1) * TOK], w[:, a, k, m * P:(m + 1) * P], src[:, b, k, :],
                                                start=False, stop=(n == len(terms) - 1))
                return last

            def project(dst, src, w, bias=None):
                for i in range(PAIR):
                    o = dst[:, i * E:(i + 1) * E]
                    if bias is not None:
                        nc.tensor.matmul(o, ones_wide[:, 0:P], bias[:], start=True, stop=False)
                    terms = [(k, a, b) for k in range(KT) for a, b in PARTS]
                    for n, (k, a, b) in enumerate(terms):
                        last = nc.tensor.matmul(o, src[:, a, k, i * P:(i + 1) * P], w[:, b, k, :],
                                                start=(n == 0 and bias is None), stop=(n == len(terms) - 1))
                return last

            def setup(stage):
                turned, product = ps_attT[0][:].rearrange("p a b -> p (a b)"), ps_attT[1][:].rearrange("p a b -> p (a b)")

                def transpose_w(w):
                    for k in range(KT):
                        for j in range(KT):
                            last = nc.tensor.transpose(turned[:, j * E + k * P:j * E + (k + 1) * P], w[:, k, j * P:(j + 1) * P], ident[:])
                    last.then_inc(setup_pe, 1)

                def multiply(rhs):
                    for m in range(KT):
                        for k in range(KT):
                            last = nc.tensor.matmul(product[:, m * E:(m + 1) * E], wT_s[:, k, m * P:(m + 1) * P], rhs[:, k, :],
                                                    start=(k == 0), stop=(k == KT - 1))
                    last.then_inc(setup_pe, 1)

                if stage == 0:
                    pe.wait_ge(later_landed, LATER)
                    transpose_w(w2_s)
                if stage == 1:
                    pe.wait_ge(setup_dve, W2_T)
                    multiply(w3_s)
                if stage == 2:
                    pe.wait_ge(setup_dve, W23)
                    transpose_w(w1_s)
                if stage == 3:
                    pe.wait_ge(setup_dve, W1_T)
                    multiply(w23_s)
                if stage == 4:
                    o = ps_a[:, 0, :]
                    nc.tensor.matmul(o, ones_row[:], bo_raw[:], start=True, stop=False)
                    for k in range(KT):
                        last = nc.tensor.matmul(o, bv_wide[:, k, :], wo_raw[:, k, :], start=False, stop=(k == KT - 1))
                    last.then_inc(setup_pe, 1)

            def scores(b, u):
                n, m, odd = u // GROUPS, u % GROUPS // 2, u % 2
                if u == 0:
                    pe.wait_ge(q_landed[b.rem % 2], b.lap(2, 16 * 4))
                    pe.wait_ge(blocks_landed[b.rem % 2], b.lap(2, 16 * 2 * HT))
                wait(pe, negs_ready, b.times(UNITS, u - 1))
                for part in range(2):
                    last = nc.tensor.matmul(ps_s[u % 2][:], q_parts[b.rem % 2][:, odd, m, n * P:(n + 1) * P],
                                            k_blocks[b.rem % 2][:, part * KT + m, odd * G:(odd + 1) * G, n * P:(n + 1) * P],
                                            start=(part == 0), stop=(part == 1))
                last.then_inc(s_done, 1)

            def transpose_weights(b, u):
                pe.wait_ge(att_ready, b.times(UNITS, u + 1))
                before = unit(b, u - 2)
                if before[0].exists():
                    pe.wait_ge(*copied(*before))
                for j in range(G):
                    last = nc.tensor.transpose(ps_attT[u % 2][:, j, :], att[u % 2][:, j, :], ident[:])
                last.then_inc(attT_done, 1)

            def weigh_values(b, u):
                n, m, odd = u // GROUPS, u % GROUPS // 2, u % 2
                if u == 0:
                    pe.wait_ge(v_ready, b.times(1, 1))
                    wait(pe, aT_ready, b.times(1, 0))
                pe.wait_ge(*copied(b, u))
                for j in range(G):
                    v = v_gap[b.rem % 2][:, n, m * G + j, odd:odd + 2, :].rearrange("p a d -> p (a d)")
                    last = nc.tensor.matmul(ps_a[j * SLOT:(j + 1) * SLOT, m, n * P:(n + 1) * P], v, attT[u % 2][:, j, :],
                                            start=(odd == 0), stop=(odd == 1), tile_position=(0, j * SLOT))
                last.then_inc(pv_done, 1)

            def body(t):
                nxt, b, c, d = t.back(-1), t.back(1), t.back(2), t.back(3)

                def ahead(u):
                    pair, unit_ahead = unit(b, u + 3)
                    if pair.exists():
                        scores(pair, unit_ahead)

                def attend(u):
                    if b.exists():
                        transpose_weights(b, u)
                    pair, unit_before = unit(b, u - 1)
                    if pair.exists():
                        weigh_values(pair, unit_before)
                    if t.known and t.n == 0:
                        setup(u)

                def step(name, pair, ready, count, work, done):
                    if pair.exists():
                        dst = bank_of(name, t)
                        pe.wait_ge(ready, count)
                        work(dst).then_inc(done, 1)

                def pair_of(src):
                    return lambda dst: transposes(dst, [src[:, i, :] for i in range(PAIR)])

                if t.known and t.n == 0:
                    pe.wait_ge(consts_ready, 3)
                    pe.wait_ge(ctx_landed[0], 16)
                    pair_of(ctx_in[0])(ps_m[BANK["cT"]]).then_inc(cT_done, 1)
                    pe.wait_ge(bias_landed, 16)
                    pe.wait_ge(cT_ready, 1)
                    pe.wait_ge(setup_dve, SETUP_Q)
                    project_T(ps_m[BANK["k"]], wk_s, cT, bqk_rows[:, 1, :]).then_inc(k_done, 1)
                    pe.wait_ge(k_ready, 1)
                    pe.wait_ge(xn_ready, PAIR)
                    pair_of(xn)(ps_m[BANK["xT"]]).then_inc(xT_done, 1)
                ahead(0)
                step("v", t, cT_ready, t.times(1, 1), lambda dst: project(dst, cT, wv_s), v_done)
                attend(0)
                ahead(1)
                step("cT", nxt, ctx_landed[nxt.rem % 2], nxt.lap(2, 16), pair_of(ctx_in[nxt.rem % 2]), cT_done)
                step("q", t, xT_ready, t.times(1, 1), lambda dst: project_T(dst, wq_s, xT, bqk_rows[:, 0, :]), q_done)
                attend(1)
                ahead(2)
                if t.known and t.n == 2:
                    pe.wait_ge(setup_dve, LATER_LOW)
                    pe.wait_ge(bias_landed, 32)
                step("o", c, aT_ready, c.times(1, 1), lambda dst: project(dst, aT, wo_s), o_done)
                attend(2)
                ahead(3)
                step("k", nxt, cT_ready, nxt.times(1, 1), lambda dst: project_T(dst, wk_s, cT, bqk_rows[:, 1, :]), k_done)
                attend(3)
                ahead(4)
                step("yT", d, yn_ready, d.times(PAIR, PAIR), pair_of(yn), yT_done)
                attend(4)
                ahead(5)
                attend(5)
                ahead(6)
                step("f", d, yT_ready, d.times(1, 1), lambda dst: project(dst, yT, wf_s, bf_rows), f_done)
                attend(6)
                ahead(7)
                step("xT", nxt, xn_ready, nxt.times(PAIR, PAIR), pair_of(xn), xT_done)
                attend(7)

            turns(pe, body)

        @block.scalar
        def _(act):
            act.wait_ge(first_landed, FIRST)
            nc.scalar.activation(tgates[:], gates[:], ACT.Tanh).then_inc(setup_act, 1)

            def flat(a):
                return a[:].rearrange("p a b -> p (a b)")

            def high(dst, src, done, count, free, freed, ready):
                act.wait_ge(done, count)
                wait(act, free, freed)
                src = src[:] if len(src.shape) == 2 else flat(src)
                nc.scalar.activation(dst[:, 0].rearrange("p k n -> p (k n)"), src, ACT.Copy).then_inc(ready, 1)

            def expo(b, u):
                act.wait_ge(negs_ready, b.times(UNITS, u + 1))
                wait(act, att_ready, b.times(UNITS, u - 3))
                for j in range(G):
                    last = nc.scalar.activation(probs[u % 4][:, j, :], negs[u % 2][:, j, :], ACT.Exp, scale=-1.0,
                                                bias=neg_max[u % 2][:, j:j + 1], accum_out=den[u % 4][:, j:j + 1])
                last.then_inc(probs_ready, 1)

            def copy_weights(b, u):
                act.wait_ge(attT_done, b.times(UNITS, u + 1))
                wait(act, pv_done, b.times(UNITS, u - 1))
                nc.scalar.activation(flat(attT[u % 2]), flat(ps_attT[u % 2]), ACT.Copy).then_inc(attT_by_act, 1)

            def high_of_ctx(p):
                high(cT, ps_m[BANK["cT"]], cT_done, p.times(1, 1), v_done, p.times(1, 0), cT_high)

            def high_of_k(p):
                if not p.known or p.n > 0:
                    act.wait_ge(blocks_landed[(p.rem - 1) % 2], p.back(1).lap(2, 16 * 2 * HT))
                high(kT, ps_m[BANK["k"]], k_done, p.times(1, 1), cT_ready, p.times(1, 0), k_high)

            def high_of_q(p):
                if not p.known or p.n > 0:
                    act.wait_ge(q_landed[(p.rem - 1) % 2], p.back(1).lap(2, 16 * 4))
                high(qT, ps_m[BANK["q"]], q_done, p.times(1, 1), xT_ready, p.times(1, 0), q_high)

            def high_of_x(p):
                high(xT, ps_m[BANK["xT"]], xT_done, p.times(1, 1), q_done, p.times(1, 0), xT_high)

            def body(t):
                nxt, b, c, d = t.back(-1), t.back(1), t.back(2), t.back(3)
                if t.known and t.n == 0:
                    high_of_ctx(t)
                    high_of_k(t)
                    high_of_x(t)
                for u in range(UNITS):
                    if u == 1 and c.exists():
                        high(aT, ps_a, pv_done, c.times(UNITS, UNITS), o_done, c.times(1, 0), aT_high)
                    if unit(b, u - 1)[0].exists() and (u - 1) % UNITS in BY_ACT:
                        copy_weights(*unit(b, u - 1))
                    if u == 2 and t.exists():
                        high_of_q(t)
                    if u == 7 and d.exists():
                        act.wait_ge(f_done, d.times(1, 1))
                        wait(act, gated, d.times(1, 0))
                        nc.scalar.activation(flat(th), ps_m[BANK["f"]][:], ACT.Tanh).then_inc(th_ready, 1)
                    if unit(b, u + 2)[0].exists():
                        expo(*unit(b, u + 2))
                    if u == 0 and t.exists():
                        act.wait_ge(v_done, t.times(1, 1))
                        wait(act, pv_done, t.times(UNITS, -UNITS))
                        nc.scalar.activation(v_gap[t.rem % 2][:, :, :, 0:3:2, :].rearrange("p b a z d -> p (b a) z d"),
                                             ps_m[BANK["v"]][:].rearrange("p (a z d) -> p a z d", z=2, d=D), ACT.Copy).then_inc(v_ready, 1)
                    if u == 1 and nxt.exists():
                        high_of_ctx(nxt)
                    if u == 4 and nxt.exists():
                        high_of_k(nxt)
                    if u == 4 and d.exists():
                        high(yT, ps_m[BANK["yT"]], yT_done, d.times(1, 1), f_done, d.times(1, 0), yT_high)
                    if u == 7 and nxt.exists():
                        high_of_x(nxt)

            turns(act, body)

        @block.vector
        def _(dve):
            def flat(a):
                return a.rearrange("p k n -> p (k n)")

            def setup_first():
                dve.wait_ge(first_landed, FIRST)

                def sort(dst, src, odd):
                    return (dst.rearrange("p k (m z f) -> p (k m) z f", m=KT, z=2)[:, :, odd, :].rearrange("p a (j d) -> p a j d", d=D),
                            src.rearrange("p k (m j z d) -> p (k m) j z d", m=KT, z=2, d=D)[:, :, :, odd, :])

                for odd in range(2):
                    nc.vector.tensor_copy(*sort(bqk_sorted[:, 1:2, :], bqk_raw[:, 1:2, :], odd))
                    last = nc.vector.tensor_scalar(*sort(bqk_sorted[:, 0:1, :], bqk_raw[:, 0:1, :], odd), -float(D) ** -0.5, None, ALU.mult)
                    nc.vector.tensor_copy(*sort(wk_sorted[:], wk_raw[:], odd))
                    last = nc.vector.tensor_scalar(*sort(wq_neg[:], wq_raw[:], odd), -float(D) ** -0.5, None, ALU.mult)
                last.then_inc(setup_dve, 1)
                dve.wait_ge(setup_dve, SORTED)
                dve.wait_ge(consts_ready, 2)
                nc.vector.tensor_copy(bqk_rows[0:1, :, :], bqk_sorted[:])
                nc.vector.tensor_copy(bv_wide[:], bv_s[:].unsqueeze(2).to_broadcast([P, KT, P]))
                for dst, src in ((wk_s, wk_sorted), (wv_s, wv_raw)):
                    last = nc.vector.tensor_copy(flat(dst[:, 0]), flat(src[:]))
                last.then_inc(setup_dve, 1)
                dve.wait_ge(setup_dve, SETUP_HIGH)
                nc.vector.tensor_tensor(bqk_low[:], bqk_sorted[:], bqk_rows[0:1, :, :], ALU.subtract).then_inc(setup_dve, 1)
                nc.vector.tensor_copy(flat(wq_s[:, 0]), flat(wq_neg[:]))
                for dst, src in ((wk_s, wk_sorted), (wv_s, wv_raw)):
                    last = nc.vector.tensor_tensor(flat(dst[:, 1]), flat(src[:]), flat(dst[:, 0]), ALU.subtract)
                last.then_inc(setup_dve, 1)
                dve.wait_ge(setup_dve, SETUP_LOW)
                nc.vector.tensor_scalar(far[:], mask_i[:], 0, FAR, ALU.is_equal, ALU.mult)
                nc.vector.tensor_tensor(flat(wq_s[:, 1]), flat(wq_neg[:]), flat(wq_s[:, 0]), ALU.subtract).then_inc(setup_dve, 1)

            def setup_products(stage):
                if stage < 4:
                    dst, src = ((wT_s, ps_attT[0]), (w23_s, ps_attT[1]), (wT_s, ps_attT[0]), (w123_s, ps_attT[1]))[stage]
                    dve.wait_ge(setup_pe, stage + 1)
                    nc.vector.tensor_copy(flat(dst[:]), flat(src[:])).then_inc(setup_dve, 1)
                if stage == 4:
                    dve.wait_ge(setup_act, 1)
                    dve.wait_ge(setup_pe, 5)
                    nc.vector.tensor_scalar(flat(wo_g[:]), flat(wo_raw[:]), tgates[:, 0:1], None, ALU.mult)
                    nc.vector.tensor_scalar(bo_g[:], ps_a[:, 0, :], tgates[:, 0:1], None, ALU.mult).then_inc(setup_dve, 1)

            def setup_later(stage):
                weights = ((wo_s, wo_g), (wf_s, w123_s))
                if stage == 0:
                    dve.wait_ge(setup_dve, OUT_BIAS)
                    nc.vector.tensor_copy(bf_rows[0:1, :], bf_raw[:])
                    for dst, src in weights:
                        last = nc.vector.tensor_copy(flat(dst[:, 0]), flat(src[:]))
                    last.then_inc(setup_dve, 1)
                if stage == 1:
                    dve.wait_ge(setup_dve, LATER_HIGH)
                    nc.vector.tensor_tensor(bf_low[:], bf_raw[:], bf_rows[0:1, :], ALU.subtract).then_inc(setup_dve, 1)
                    for dst, src in weights:
                        last = nc.vector.tensor_tensor(flat(dst[:, 1]), flat(src[:]), flat(dst[:, 0]), ALU.subtract)
                    last.then_inc(setup_dve, 1)

            def maxima(b, u):
                for j in range(G):
                    last = nc.vector.tensor_tensor_reduce(out=negs[u % 2][:, j, :], in0=ps_s[u % 2][:, j, :], in1=far[:], scale=1.0,
                                                          scalar=2 * FAR, op0=ALU.add, op1=ALU.min, accum_out=neg_max[u % 2][:, j:j + 1])
                last.then_inc(negs_ready, 1)

            def reciprocals(b, u):
                dve.wait_ge(probs_ready, b.times(UNITS, u + 1))
                nc.vector.reciprocal(den_r[u % 4][:], den[u % 4][:]).then_inc(den_ready, 1)

            def copy_weights(b, u):
                dve.wait_ge(attT_done, b.times(UNITS, u + 1))
                wait(dve, pv_done, b.times(UNITS, u - 1))
                nc.vector.tensor_copy(flat(attT[u % 2][:]), flat(ps_attT[u % 2][:])).then_inc(attT_by_dve, 1)

            def low(dst, src, high_ready, count, ready):
                dve.wait_ge(high_ready, count)
                src = src[:] if len(src.shape) == 2 else flat(src[:])
                nc.vector.tensor_tensor(flat(dst[:, 1]), src, flat(dst[:, 0]), ALU.subtract).then_inc(ready, 1)

            def low_of_ctx(p):
                low(cT, ps_m[BANK["cT"]], cT_high, p.times(1, 1), cT_ready)

            def low_of_k(p):
                wait(dve, s_done, p.times(UNITS, -UNITS))
                low(kT, ps_m[BANK["k"]], k_high, p.times(1, 1), k_ready)

            def low_of_x(p):
                low(xT, ps_m[BANK["xT"]], xT_high, p.times(1, 1), xT_ready)

            def stats(which, src):
                for i in range(PAIR):
                    last = nc.vector.bn_stats(stat6[:, which, i, :], src[:, i, :])
                last.then_inc(dve_step, 1)

            def moments(which, ready):
                for i in range(PAIR):
                    last = nc.vector.bn_aggr(stat2[:, which, i, :], stat6[:, which, i, :])
                last.then_inc(ready, 1)

            def stats_of_x(p):
                dve.wait_ge(x_landed[p.rem], p.lap(BODY, 16))
                wait(dve, xn_ready, p.times(PAIR, 0))
                stats(0, x_in[p.rem])

            def body(t):
                nxt, b, c, d = t.back(-1), t.back(1), t.back(2), t.back(3)
                first, x_pair = t.known and t.n == 0, t.back(-2)
                taken = min(t.n + 2, NP) + max(0, t.n - 2) if t.known else t.times(2, 0)

                if t.known and t.n == 0:
                    nc.vector.memset(stat2[:].rearrange("p a b c -> p (a b c)"), 1.0)
                    stats_of_x(t)
                    dve.wait_ge(dve_step, 1)
                    moments(0, stat1_ready)
                    setup_first()
                    low_of_ctx(t)
                    low_of_k(t)
                    low_of_x(t)
                for u in range(UNITS):
                    x_taken, y_taken = u == 7 and x_pair.exists(), u == 4 and c.exists()
                    coming, summed, behind = unit(b, u + 2), unit(b, u + 1), unit(b, u - 1)
                    if coming[0].exists():
                        dve.wait_ge(s_done, coming[0].times(UNITS, coming[1] + 1))
                        dve.sem_inc(scores_seen, 1)
                        maxima(*coming)
                    if behind[0].exists() and behind[1] in BY_DVE:
                        copy_weights(*behind)
                    if x_taken or y_taken:
                        taken = taken + 1
                        dve.wait_ge(dve_step, taken)
                    if summed[0].exists():
                        reciprocals(*summed)
                    if x_taken:
                        moments(0, stat1_ready)
                    if y_taken:
                        moments(1, stat2_ready)
                    if u == 1 and c.exists():
                        low(aT, ps_a, aT_high, c.times(1, 1), aT_ready)
                    if u == 0 and t.exists() and not (t.known and t.n == 0):
                        low_of_x(t)
                    if u == 0 and first:
                        stats_of_x(nxt)
                        dve.wait_ge(dve_step, 2)
                        moments(0, stat1_ready)
                    if u == 6 and x_pair.exists():
                        stats_of_x(x_pair)
                    if u == 2 and t.exists():
                        low(qT, ps_m[BANK["q"]], q_high, t.times(1, 1), q_ready)
                    if u == 2 and nxt.exists():
                        low_of_ctx(nxt)
                    if u == 3 and c.exists():
                        dve.wait_ge(x_biased, c.times(1, 1))
                        dve.wait_ge(y_free[c.rem], c.lap(BODY, 16))
                        dve.wait_ge(o_done, c.times(1, 1))
                        nc.vector.tensor_tensor(flat(y[c.rem][:]), ps_m[BANK["o"]][:], flat(x_in[c.rem][:]),
                                                ALU.add).then_inc(y_ready, 1)
                        if c.known and c.n == 0:
                            dve.wait_ge(xn_ready, nxt.times(PAIR, PAIR))
                        wait(dve, yn_ready, c.times(PAIR, 0))
                        dve.wait_ge(y_ready, c.times(1, 1))
                        stats(1, y[c.rem])
                    if u == 5 and nxt.exists():
                        low_of_k(nxt)
                    if u == 5 and d.exists():
                        low(yT, ps_m[BANK["yT"]], yT_high, d.times(1, 1), yT_ready)
                    if t.known and t.n == 0:
                        setup_products(u)
                    if t.known and t.n == 1 and u in (3, 4):
                        setup_later(u - 3)

            turns(dve, body)


_INS = ["x", "ctx_1024", "mask_1x1xSxS2_ik0", "g_xattn", "g_ffn", "L0_xattn_Wv", "L0_xattn_bv", "L0_xattn_Wk",
        "L0_xattn_bk", "L0_xattn_Wq", "L0_xattn_bq", "L0_xattn_Wo", "L0_xattn_bo", "L0_ffn_weight",
        "L0_ffn_aux_weight1", "L0_ffn_aux_weight2", "L0_ffn_bias"]


def kernel(**inputs):
    import numpy as np
    import concourse.bacc as bacc
    from concourse.bass_utils import run_bass_kernel_spmd

    nc = bacc.Bacc("TRN2", target_bir_lowering=False, num_devices=1)
    arrays, args = {}, []
    for name in _INS:
        a = np.ascontiguousarray(inputs[name])
        arrays[f"in_{name}"] = a
        args.append(nc.dram_tensor(f"in_{name}", a.shape, mybir.dt.from_np(a.dtype), kind="ExternalInput").ap())
    shape = np.shape(inputs["x"])
    args.append(nc.dram_tensor("out_0", shape, F32, kind="ExternalOutput").ap())
    gated_xattn_block(nc, *args)
    r = run_bass_kernel_spmd(nc, [arrays], core_ids=[0])
    return r.results[0]["out_0"]
```
